# Optimizing a Trainium2 kernel written in Bass

```python
import numpy as np
import jax
import jax.numpy as jnp

def _softmax(x, axis=-1):
    return jax.nn.softmax(x, axis=axis)

def _gelu(x):
    return jax.nn.gelu(x, approximate=True)

def _silu(x):
    return jax.nn.silu(x)

def _sigmoid(x):
    return jax.nn.sigmoid(x)

def _layernorm(x, axis=-1, eps=1e-05):
    m = jnp.mean(x, axis=axis, keepdims=True)
    v = jnp.var(x, axis=axis, keepdims=True)
    return (x - m) / jnp.sqrt(v + eps)

def _scatter_add(tgt, idx, src, axis=0):
    return tgt.at[idx].add(src)

def _segment_sum(src, seg, n):
    return jax.ops.segment_sum(src, seg, n)
kernel_name = 'mk_recurrent_d1_jaxref_r8_d7aa6b'

def setup_inputs(seed: int=0):
    np.random.seed(seed)
    _w = jnp.asarray

    def _L0_attn_setup():
        import jax, jax.numpy as jnp
        import numpy as np
        EPS = 1e-06

        def _causal_depthwise_conv(x, conv_w, conv_b):
            B, L, d = x.shape
            lhs = jnp.transpose(x, (0, 2, 1))
            out = jax.lax.conv_general_dilated(lhs, conv_w, window_strides=(1,), padding=[(3, 0)], feature_group_count=d, dimension_numbers=('NCH', 'OIH', 'NCH'))
            out = out + conv_b[None, :, None]
            return jnp.transpose(out, (0, 2, 1))
        key = jax.random.key(seed)
        ks = jax.random.split(key, 8)
        B, L, d = (4, 512, 128)
        x = jax.random.normal(ks[0], (B, L, d), dtype=jnp.float32)
        conv_w = jax.random.normal(ks[1], (d, 1, 4), dtype=jnp.float32) * 0.02
        conv_b = jnp.zeros((d,), dtype=jnp.float32)
        lim = 1.0 / np.sqrt(d)
        W_r = jax.random.uniform(ks[2], (d, d), jnp.float32, -lim, lim)
        b_r = jax.random.uniform(ks[3], (d,), jnp.float32, -lim, lim)
        W_i = jax.random.uniform(ks[4], (d, d), jnp.float32, -lim, lim)
        b_i = jax.random.uniform(ks[5], (d,), jnp.float32, -lim, lim)
        log_a = jnp.full((d,), 7.5, dtype=jnp.float32)
        W_out = jax.random.uniform(ks[6], (d, d), jnp.float32, -lim, lim)
        gamma = jnp.ones((d,), dtype=jnp.float32)
        return {'x': x, 'conv_w': conv_w, 'conv_b': conv_b, 'W_r': W_r, 'b_r': b_r, 'W_i': W_i, 'b_i': b_i, 'log_a': log_a, 'W_out': W_out, 'gamma': gamma}
    _L0_attn_in = _L0_attn_setup()

    def _L0_ffn_setup():
        import jax, jax.numpy as jnp
        import numpy as np
        DIM = 128
        DEPTH = 2
        HEADS = 8
        DIM_HEAD = 64
        WINDOW = 64
        INNER = HEADS * DIM_HEAD
        HID = int(DIM * 4 * 2 / 3)
        B, N = (2, 1024)
        QK_SCALE = 8.0

        def shift_token(t):
            t1, t2 = jnp.split(t, 2, axis=-1)
            t2 = jnp.pad(t2, ((0, 0), (1, 0), (0, 0)))[:, :-1]
            return jnp.concatenate([t1, t2], axis=-1)

        def l2norm(t):
            return t / jnp.clip(jnp.linalg.norm(t, axis=-1, keepdims=True), 1e-12)

        def rotate_half(x):
            x1, x2 = jnp.split(x, 2, axis=-1)
            return jnp.concatenate([-x2, x1], axis=-1)

        def rotary_xpos(q, k):
            n = q.shape[-2]
            half_idx = jnp.arange(0, DIM_HEAD, 2, dtype=jnp.float32)
            inv_freq = 1.0 / 10000.0 ** (half_idx / DIM_HEAD)
            t = jnp.arange(n, dtype=jnp.float32)
            freqs = t[:, None] * inv_freq[None, :]
            freqs = jnp.concatenate([freqs, freqs], axis=-1)
            base = (half_idx + 0.4 * DIM_HEAD) / (1.4 * DIM_HEAD)
            power = (t - n // 2) / float(WINDOW // 2)
            scale = base[None, :] ** power[:, None]
            scale = jnp.concatenate([scale, scale], axis=-1)
            cos, sin = (jnp.cos(freqs), jnp.sin(freqs))
            q = q * cos * scale + rotate_half(q) * sin * scale
            k = k * cos / scale + rotate_half(k) * sin / scale
            return (q, k)

        def local_attention(q, k, v):
            b, h, n, d = q.shape
            w = n // WINDOW
            bq = q.reshape(b, h, w, WINDOW, d) * QK_SCALE
            bk = k.reshape(b, h, w, WINDOW, d)
            bv = v.reshape(b, h, w, WINDOW, d)

            def look_around(t):
                p = jnp.pad(t, ((0, 0), (0, 0), (1, 0), (0, 0), (0, 0)))
                return jnp.concatenate([p[:, :, :w], p[:, :, 1:]], axis=3)
            bk, bv = (look_around(bk), look_around(bv))
            bt = jnp.arange(n).reshape(w, WINDOW)
            btp = jnp.pad(bt, ((1, 0), (0, 0)), constant_values=-1)
            btk = jnp.concatenate([btp[:w], btp[1:]], axis=1)
            sim = jnp.einsum('bhwid,bhwjd->bhwij', bq, bk)
            i = bt[:, :, None]
            j = btk[:, None, :]
            mask = (i < j) | (i > j + WINDOW) | (j == -1)
            sim = jnp.where(mask, -jnp.finfo(sim.dtype).max, sim)
            attn = jax.nn.softmax(sim, axis=-1)
            out = jnp.einsum('bhwij,bhwjd->bhwid', attn, bv)
            return out.reshape(b, h, n, d)

        def _layer(x, wqkv, qs, ksc, wo, lg, lb, w1, b1, w2, b2):
            b, n, _ = x.shape
            h = shift_token(x)
            qkv = h @ wqkv
            q, k, v = jnp.split(qkv, 3, axis=-1)
            to_heads = lambda t: t.reshape(b, n, HEADS, DIM_HEAD).transpose(0, 2, 1, 3)
            q, k, v = (to_heads(q), to_heads(k), to_heads(v))
            q = l2norm(q) * qs
            k = l2norm(k) * ksc
            q, k = rotary_xpos(q, k)
            o = local_attention(q, k, v)
            o = o.transpose(0, 2, 1, 3).reshape(b, n, INNER)
            x = x + o @ wo
            h = shift_token(x)
            mu = h.mean(-1, keepdims=True)
            var = h.var(-1, keepdims=True)
            h = (h - mu) / jnp.sqrt(var + 1e-05) * lg + lb
            h = h @ w1 + b1
            a, g = jnp.split(h, 2, axis=-1)
            h = a * jax.nn.gelu(g, approximate=False)
            x = x + h @ w2 + b2
            return x
        key = jax.random.key(seed)
        ks = jax.random.split(key, 6)
        return {'x': jax.random.normal(ks[0], (B, N, DIM), jnp.float32), 'wqkv': jax.random.normal(ks[1], (DEPTH, DIM, 3 * INNER), jnp.float32) * 0.02, 'q_scale': jnp.ones((DEPTH, DIM_HEAD), jnp.float32), 'k_scale': jnp.ones((DEPTH, DIM_HEAD), jnp.float32), 'wo': jax.random.normal(ks[2], (DEPTH, INNER, DIM), jnp.float32) * 0.02, 'ln_g': jnp.ones((DEPTH, DIM), jnp.float32), 'ln_b': jnp.zeros((DEPTH, DIM), jnp.float32), 'w1': jax.random.normal(ks[3], (DEPTH, DIM, 2 * HID), jnp.float32) * 0.02, 'b1': jnp.zeros((DEPTH, 2 * HID), jnp.float32), 'w2': jax.random.normal(ks[4], (DEPTH, HID, DIM), jnp.float32) * 0.02, 'b2': jnp.zeros((DEPTH, DIM), jnp.float32)}
    _L0_ffn_in = _L0_ffn_setup()
    _d = {'L0_attn_x': _L0_attn_in['x'], 'L0_attn_conv_w': _L0_attn_in['conv_w'], 'L0_attn_conv_b': _L0_attn_in['conv_b'], 'L0_attn_W_r': _L0_attn_in['W_r'], 'L0_attn_b_r': _L0_attn_in['b_r'], 'L0_attn_W_i': _L0_attn_in['W_i'], 'L0_attn_b_i': _L0_attn_in['b_i'], 'L0_attn_log_a': _L0_attn_in['log_a'], 'L0_attn_W_out': _L0_attn_in['W_out'], 'L0_attn_gamma': _L0_attn_in['gamma'], 'L0_ffn_wqkv': _L0_ffn_in['wqkv'], 'L0_ffn_q_scale': _L0_ffn_in['q_scale'], 'L0_ffn_k_scale': _L0_ffn_in['k_scale'], 'L0_ffn_wo': _L0_ffn_in['wo'], 'L0_ffn_ln_g': _L0_ffn_in['ln_g'], 'L0_ffn_ln_b': _L0_ffn_in['ln_b'], 'L0_ffn_w1': _L0_ffn_in['w1'], 'L0_ffn_b1': _L0_ffn_in['b1'], 'L0_ffn_w2': _L0_ffn_in['w2'], 'L0_ffn_b2': _L0_ffn_in['b2']}
    _x0 = _d['L0_attn_x']
    _d['L0_attn_x'] = jax.random.normal(jax.random.fold_in(jax.random.key(seed), 1), (16, 512, 128), dtype=_x0.dtype)
    del _x0
    return _d

def reference(L0_attn_x, L0_attn_conv_w, L0_attn_conv_b, L0_attn_W_r, L0_attn_b_r, L0_attn_W_i, L0_attn_b_i, L0_attn_log_a, L0_attn_W_out, L0_attn_gamma, L0_ffn_wqkv, L0_ffn_q_scale, L0_ffn_k_scale, L0_ffn_wo, L0_ffn_ln_g, L0_ffn_ln_b, L0_ffn_w1, L0_ffn_b1, L0_ffn_w2, L0_ffn_b2):

    def _L0_attn_ref(x, conv_w, conv_b, W_r, b_r, W_i, b_i, log_a, W_out, gamma):
        import jax, jax.numpy as jnp
        import numpy as np
        EPS = 1e-06

        def _causal_depthwise_conv(x, conv_w, conv_b):
            B, L, d = x.shape
            lhs = jnp.transpose(x, (0, 2, 1))
            out = jax.lax.conv_general_dilated(lhs, conv_w, window_strides=(1,), padding=[(3, 0)], feature_group_count=d, dimension_numbers=('NCH', 'OIH', 'NCH'))
            out = out + conv_b[None, :, None]
            return jnp.transpose(out, (0, 2, 1))
        B, L, d = x.shape
        x_conv = _causal_depthwise_conv(x, conv_w, conv_b)
        r_t = jax.nn.sigmoid(x_conv @ W_r.T + b_r)
        i_t = jax.nn.sigmoid(x_conv @ W_i.T + b_i)
        a_base = jax.nn.sigmoid(log_a)
        a_t = a_base[None, None, :] ** (8.0 * r_t)
        inp = i_t * x_conv
        scale = jnp.sqrt(jnp.clip(1.0 - a_t * a_t, 0.0))

        def step(h, ab):
            a, b = ab
            h = a * h + b
            return (h, h)
        xs = (jnp.moveaxis(a_t, 1, 0), jnp.moveaxis(scale * inp, 1, 0))
        h0 = jnp.zeros((B, d), dtype=x.dtype)
        _, hs = jax.lax.scan(step, h0, xs)
        out = jnp.moveaxis(hs, 0, 1)
        out = out @ W_out.T
        rms = jax.lax.rsqrt(jnp.mean(out * out, axis=-1, keepdims=True) + EPS)
        return out * rms * gamma

    def _L0_ffn_ref(x, wqkv, q_scale, k_scale, wo, ln_g, ln_b, w1, b1, w2, b2):
        import jax, jax.numpy as jnp
        import numpy as np
        DIM = 128
        DEPTH = 2
        HEADS = 8
        DIM_HEAD = 64
        WINDOW = 64
        INNER = HEADS * DIM_HEAD
        HID = int(DIM * 4 * 2 / 3)
        B, N = (2, 1024)
        QK_SCALE = 8.0

        def shift_token(t):
            t1, t2 = jnp.split(t, 2, axis=-1)
            t2 = jnp.pad(t2, ((0, 0), (1, 0), (0, 0)))[:, :-1]
            return jnp.concatenate([t1, t2], axis=-1)

        def l2norm(t):
            return t / jnp.clip(jnp.linalg.norm(t, axis=-1, keepdims=True), 1e-12)

        def rotate_half(x):
            x1, x2 = jnp.split(x, 2, axis=-1)
            return jnp.concatenate([-x2, x1], axis=-1)

        def rotary_xpos(q, k):
            n = q.shape[-2]
            half_idx = jnp.arange(0, DIM_HEAD, 2, dtype=jnp.float32)
            inv_freq = 1.0 / 10000.0 ** (half_idx / DIM_HEAD)
            t = jnp.arange(n, dtype=jnp.float32)
            freqs = t[:, None] * inv_freq[None, :]
            freqs = jnp.concatenate([freqs, freqs], axis=-1)
            base = (half_idx + 0.4 * DIM_HEAD) / (1.4 * DIM_HEAD)
            power = (t - n // 2) / float(WINDOW // 2)
            scale = base[None, :] ** power[:, None]
            scale = jnp.concatenate([scale, scale], axis=-1)
            cos, sin = (jnp.cos(freqs), jnp.sin(freqs))
            q = q * cos * scale + rotate_half(q) * sin * scale
            k = k * cos / scale + rotate_half(k) * sin / scale
            return (q, k)

        def local_attention(q, k, v):
            b, h, n, d = q.shape
            w = n // WINDOW
            bq = q.reshape(b, h, w, WINDOW, d) * QK_SCALE
            bk = k.reshape(b, h, w, WINDOW, d)
            bv = v.reshape(b, h, w, WINDOW, d)

            def look_around(t):
                p = jnp.pad(t, ((0, 0), (0, 0), (1, 0), (0, 0), (0, 0)))
                return jnp.concatenate([p[:, :, :w], p[:, :, 1:]], axis=3)
            bk, bv = (look_around(bk), look_around(bv))
            bt = jnp.arange(n).reshape(w, WINDOW)
            btp = jnp.pad(bt, ((1, 0), (0, 0)), constant_values=-1)
            btk = jnp.concatenate([btp[:w], btp[1:]], axis=1)
            sim = jnp.einsum('bhwid,bhwjd->bhwij', bq, bk)
            i = bt[:, :, None]
            j = btk[:, None, :]
            mask = (i < j) | (i > j + WINDOW) | (j == -1)
            sim = jnp.where(mask, -jnp.finfo(sim.dtype).max, sim)
            attn = jax.nn.softmax(sim, axis=-1)
            out = jnp.einsum('bhwij,bhwjd->bhwid', attn, bv)
            return out.reshape(b, h, n, d)

        def _layer(x, wqkv, qs, ksc, wo, lg, lb, w1, b1, w2, b2):
            b, n, _ = x.shape
            h = shift_token(x)
            qkv = h @ wqkv
            q, k, v = jnp.split(qkv, 3, axis=-1)
            to_heads = lambda t: t.reshape(b, n, HEADS, DIM_HEAD).transpose(0, 2, 1, 3)
            q, k, v = (to_heads(q), to_heads(k), to_heads(v))
            q = l2norm(q) * qs
            k = l2norm(k) * ksc
            q, k = rotary_xpos(q, k)
            o = local_attention(q, k, v)
            o = o.transpose(0, 2, 1, 3).reshape(b, n, INNER)
            x = x + o @ wo
            h = shift_token(x)
            mu = h.mean(-1, keepdims=True)
            var = h.var(-1, keepdims=True)
            h = (h - mu) / jnp.sqrt(var + 1e-05) * lg + lb
            h = h @ w1 + b1
            a, g = jnp.split(h, 2, axis=-1)
            h = a * jax.nn.gelu(g, approximate=False)
            x = x + h @ w2 + b2
            return x
        for l in range(DEPTH):
            x = _layer(x, wqkv[l], q_scale[l], k_scale[l], wo[l], ln_g[l], ln_b[l], w1[l], b1[l], w2[l], b2[l])
        return x
    x = L0_attn_x
    xn = _layernorm(x, axis=-1)
    s = _L0_attn_ref(xn, L0_attn_conv_w, L0_attn_conv_b, L0_attn_W_r, L0_attn_b_r, L0_attn_W_i, L0_attn_b_i, L0_attn_log_a, L0_attn_W_out, L0_attn_gamma)
    g = _silu(_L0_ffn_ref(xn, L0_ffn_wqkv, L0_ffn_q_scale, L0_ffn_k_scale, L0_ffn_wo, L0_ffn_ln_g, L0_ffn_ln_b, L0_ffn_w1, L0_ffn_b1, L0_ffn_w2, L0_ffn_b2))
    x = x + s * g
    return x

_drawn_inputs = setup_inputs


def setup_inputs(seed=0):
    import zlib

    import numpy as np

    out = dict(_drawn_inputs(seed))
    spreads = {'L0_attn_conv_b': (0.0, 0.1),
     'L0_attn_log_a': (7.5, 0.2),
     'L0_attn_gamma': (1.0, 0.2),
     'L0_ffn_q_scale': (1.0, 0.6),
     'L0_ffn_k_scale': (1.0, 0.6),
     'L0_ffn_ln_g': (1.0, 0.6),
     'L0_ffn_ln_b': (0.0, 0.8),
     'L0_ffn_b1': (0.0, 0.8),
     'L0_ffn_b2': (0.0, 0.369)}
    factors = {'L0_attn_W_r': 8.0,
     'L0_attn_b_r': 8.0,
     'L0_attn_W_i': 3.388,
     'L0_attn_b_i': 3.399,
     'L0_ffn_wqkv': 3.508,
     'L0_ffn_wo': 3.488,
     'L0_ffn_w1': 5.745,
     'L0_ffn_w2': 5.612}
    for name, (base, spread) in spreads.items():
        noise = np.random.default_rng([zlib.crc32(name.encode()), seed]).standard_normal(out[name].shape)
        drawn = base * np.exp(spread * noise) if base else spread * noise
        out[name] = jnp.asarray(drawn.astype(out[name].dtype))
    for name, factor in factors.items():
        out[name] = (out[name] * factor).astype(out[name].dtype)
    return out
```

```python
from contextlib import ExitStack

import numpy as np

import concourse.bass as bass
from concourse import mybir

F32 = mybir.dt.float32
BF16 = mybir.dt.bfloat16
ALU = mybir.AluOpType
ACT = mybir.ActivationFunctionType
AX = mybir.AxisListType.X

NB, L, D = 16, 512, 128
TPB = L // 128
NT = NB * TPB
DEPTH, HEADS, DH, WIN = 2, 8, 64, 64
INNER = HEADS * DH
HID = 341
CH = [(0, 128), (128, 128), (256, 85)]
LN_EPS = 1e-5
RMS_EPS = 1e-6
LN2 = 0.6931471805599453


class Queue:

    def __init__(self, sem):
        self.sem, self.items, self.count, self.seen, self.last = sem, [], 0, {}, None

    def wait(self, *toks):
        for t in toks:
            if t is not None and self.seen.get(id(t[0]), 0) < t[1]:
                self.seen[id(t[0])] = t[1]
                self.items.append(lambda e, t=t: e.wait_ge(t[0], t[1]))

    def put(self, ins):
        self.items.append(ins)

    def run(self, ins, *waits):
        self.wait(*waits)
        self.count += 1
        self.last = (self.sem, self.count)
        self.items.append(lambda e: ins(e).then_inc(self.sem, 1))
        return self.last

    def emit(self, e):
        for i in self.items:
            i(e)


class Dma:

    def __init__(self, sem):
        self.sem, self.count = sem, 0

    def start(self, q, out, in_, *waits):
        q.wait(*waits)
        self.count += 16
        q.put(lambda e: e.dma_start(out, in_).then_inc(self.sem, 16))
        return (self.sem, self.count)


def mm(out, lhsT, rhs, start=True, stop=True):
    return lambda e: e.matmul(out, lhsT, rhs, start=start, stop=stop, skip_group_check=True)


def tr(out, in_, ident):
    return lambda e: e.transpose(out, in_, ident)


def act(out, in_, f, **kw):
    return lambda e: e.activation(out, in_, f, **kw)


def tt(out, a, b, op):
    return lambda e: e.tensor_tensor(out, a, b, op)


def ts(out, a, s1, s2, op0, op1=None):
    if op1 is None:
        return lambda e: e.tensor_scalar(out, a, s1, None, op0)
    return lambda e: e.tensor_scalar(out, a, s1, s2, op0, op1)


def stt(out, a, s, b, op0, op1):
    return lambda e: e.scalar_tensor_tensor(out, a, s, b, op0, op1)


def cp(out, a):
    return lambda e: e.tensor_copy(out, a)


def zero(out, v=0.0):
    return lambda e: e.memset(out, v)


def program(nc, d, out):
    ctx = ExitStack()
    with ctx:
        def sb(name, shape, dt=F32):
            return ctx.enter_context(nc.sbuf_tensor(name, shape, dt))

        def sem(name):
            return ctx.enter_context(nc.semaphore(name))

        pe, sc, ve, po, sp = (Queue(sem(n)) for n in ("s_pe", "s_act", "s_dve", "s_pool", "s_sp"))

        X = sb("X", [128, NB * L])
        A = sb("A", [128, NB * L])
        B = sb("B", [128, NB * L])
        wqkv = sb("wqkv", [128, DEPTH, 3 * INNER])
        wo = sb("wo", [128, DEPTH, 4, 128])
        w1 = sb("w1", [128, DEPTH, 2 * HID])
        w2 = sb("w2", [128, DEPTH, 3, 128])
        wr = sb("wr", [128, 3, 128])
        tab = sb("tab", [128, 2, TPB, 2, DH])
        tabl = sb("tabl", [128, 2, TPB, 2, DH])
        qks = sb("qks", [128, 2, DEPTH, 2, DH])
        cols = sb("cols", [128, 32])
        gam = sb("gam", [128, 128])
        idf = sb("idf", [128, 128])
        idb = sb("idb", [128, 128], BF16)
        avg = sb("avg", [128, 128])
        mask = sb("mask", [128, 2, 512], BF16)
        cst = sb("cst", [128, 8])
        ab = sb("ab", [128, 16])
        st = sb("st", [128, 4, 6])
        mv = sb("mv", [128, NT, 2])
        rst = sb("rst", [128, NT])
        ss = sb("ss", [128, 16])
        rr = sb("rr", [128, 16])
        nm = sb("nm", [128, 8])
        den = sb("den", [128, 8])
        rden = sb("rden", [128, 8])
        t1 = sb("t1", [128, 1024])
        t2 = sb("t2", [128, 1024])
        P = sb("P", [128, 8, 128])
        PT = sb("PT", [128, 8, 128])
        qbd = sb("qbd", [128, 8, 128])
        kT = sb("kT", [128, 4, 64 + L])
        Vn = sb("Vn", [128, TPB, INNER])
        Vs = sb("Vs", [128, TPB, INNER])
        oT = sb("oT", [128, 4, L])
        hT = sb("hT", [128, 2, L])
        h2 = sb("h2", [128, L])
        sq = sb("sq", [128, L])
        rsd = sb("rsd", [128, L])
        ps = ctx.enter_context(nc.psum_tensor("ps", [128, 8, 512], F32))

        CB, BR, BI, LA, CW = (cols[:, i:i + 1] for i in range(5))
        cw = [cols[:, 4 + j:5 + j] for j in range(4)]

        def lcol(l, j):
            return cols[:, 8 + 9 * l + j:9 + 9 * l + j]

        one, eps_ln, eps_rms, ln2x8 = (cst[:, i:i + 1] for i in range(4))

        ld = Dma(sem("s_ld"))
        lw = Dma(sem("s_lw"))
        ring = [Dma(sem(f"s_x{i}")) for i in range(4)]
        xt = [t1[:, 0:512], t1[:, 512:1024], t2[:, 0:512], t2[:, 512:1024]]
        xd = d["x"].rearrange("b (t p) d -> b p t d", p=128)
        od = out.rearrange("b (t p) d -> b p t d", p=128)

        def load_x(b, *waits):
            return ring[b % 4].start(sp, xt[b % 4].rearrange("p (t d) -> p t d", t=TPB), xd[b], *waits)

        xtok = {}
        for b in range(4):
            xtok[b] = load_x(b)
        for t_, n in ((cols, "cols"), (idf, "idf"), (wr, "wr")):
            small = ld.start(sp, t_[:], d[n])
        for t_, n in ((wqkv, "wqkv"), (tab, "tab"), (idb, "idb"), (mask, "mask"), (avg, "avg"), (wo, "wo"),
                      (w1, "w1"), (w2, "w2")):
            big = lw.start(sp, t_[:], d[n])
        big = lw.start(sp, gam[:], d["gamma"].partition_broadcast(128))
        for i, n in enumerate(("q_scale", "k_scale")):
            flat = d[n].rearrange("l e -> (l e)")
            big = lw.start(sp, qks[:, i, :, 0, :], d[n].partition_broadcast(128))
            big = lw.start(sp, qks[:, i, :, 1, 0:32], d[n][:, 32:64].partition_broadcast(128))
            big = lw.start(sp, qks[:, i, :, 1, 32:64], d[n][:, 0:32].partition_broadcast(128))

        for i, v in enumerate((1.0, LN_EPS, RMS_EPS, 8 * LN2)):
            ve.run(zero(cst[:, i:i + 1], v))
        ve.run(zero(qbd[:]))
        ve.run(zero(kT[:, :, 0:64]))
        ve.run(zero(Vs[0:64, 0, :]))
        ve.run(zero(hT[64:128, :, 0:1]))
        consts = ve.run(zero(h2[64:128, 0:1]))

        def barrier():
            toks = [q.last for q in (pe, sc, ve, po) if q.last]
            for q in (pe, sc, ve, po, sp):
                q.wait(*toks)

        sc.put(lambda e: e.preload_act_table_set("natural_log_exp_and_others"))
        sc.wait(consts)
        xn = [A[:, 0:512], A[:, 512:1024]]
        xn_free = {}
        for b in range(NB):
            xb = xt[b % 4].rearrange("p (t d) -> p t d", t=TPB)
            ve.wait(xtok[b])
            for t in range(TPB):
                k = ve.run(lambda e, t=t, xb=xb: e.bn_stats(st[:, t, :], xb[:, t, :]))
            ve.wait(k)
            for t in range(TPB):
                k = ve.run(lambda e, t=t, b=b: e.bn_aggr(mv[:, b * TPB + t, :], st[:, t, :]))
            r4 = rst[:, b * TPB:(b + 1) * TPB]
            k = sc.run(act(r4, mv[:, b * TPB:(b + 1) * TPB, 1], ACT.Ln, bias=eps_ln), k)
            k = sc.run(act(r4, r4, ACT.Exp, scale=-0.5), k)
            ve.wait(k, xn_free.get(b - 2))
            for t in range(TPB):
                n = b * TPB + t
                k = ve.run(ts(xn[b % 2][:, t * 128:(t + 1) * 128], xb[:, t, :], mv[:, n, 0:1], rst[:, n:n + 1],
                              ALU.subtract, ALU.mult))
            if b + 4 < NB:
                xtok[b + 4] = load_x(b + 4, k)
            pe.wait(k, small, xn_free.get(("ps", b - 2)))
            for t in range(TPB):
                k = pe.run(tr(ps[:, b % 2, t * 128:(t + 1) * 128], xn[b % 2][:, t * 128:(t + 1) * 128], idf[:]))
            xn_free[b] = k
            xn_free["ps", b] = sc.run(act(X[:, b * L:(b + 1) * L], ps[:, b % 2, :], ACT.Copy), k)
        barrier()

        ax, ez, u, dd, lnu, ru, la8 = (ab[:, i:i + 1] for i in range(7))
        nx, mx = ab[:, 7:8], ab[:, 8:9]
        k = ve.run(ts(nx, LA, -1.0, None, ALU.mult), small)
        k = ve.run(tt(ax, LA, nx, ALU.max), k)
        k = sc.run(act(ez, ax, ACT.Exp, scale=-1.0), k)
        k = ve.run(ts(u, ez, 1.0, None, ALU.add), k)
        k2 = sc.run(act(lnu, u, ACT.Ln), k)
        k = ve.run(ts(dd, u, -1.0, None, ALU.add), k)
        k = ve.run(tt(dd, ez, dd, ALU.subtract), k)
        ve.run(ts(mx, nx, 0.0, None, ALU.max))
        k = ve.run(lambda e: e.reciprocal(ru, u), k)
        k = ve.run(stt(dd, dd, ru, lnu, ALU.mult, ALU.add), k, k2)
        k = ve.run(tt(dd, dd, mx, ALU.add), k)
        la = ve.run(ts(la8, dd, -8.0, None, ALU.mult), k)

        xc = [t1[:, 0:512], t1[:, 512:1024]]
        it = [t2[:, 0:512], t2[:, 512:1024]]
        free = {}
        for b in range(NB):
            x = X[:, b * L:(b + 1) * L]
            y = xc[b % 2]
            k = ve.run(ts(y, x, cw[3], CB, ALU.mult, ALU.add), free.get(("pe", b - 2)))
            for s in (1, 2, 3):
                k = ve.run(stt(y[:, s:], x[:, :L - s], cw[3 - s], y[:, s:], ALU.mult, ALU.add), k)
            p0, p1 = 2 * (b % 2), 2 * (b % 2) + 1
            k1 = pe.run(mm(ps[:, p0, :], wr[:, 0, :], y), k, free.get(("r", b - 2)))
            k2 = pe.run(mm(ps[:, p1, :], wr[:, 1, :], y), free.get(("i", b - 2)))
            free["pe", b] = k2
            free["r", b] = sc.run(act(A[:, b * L:(b + 1) * L], ps[:, p0, :], ACT.Sigmoid, bias=BR), k1)
            k = sc.run(act(it[b % 2], ps[:, p1, :], ACT.Sigmoid, bias=BI), k2, free.get(("dv", b - 2)))
            free["i", b] = k
            free["dv", b] = ve.run(tt(B[:, b * L:(b + 1) * L], it[b % 2], y, ALU.mult), k)
        barrier()
        sc.put(lambda e: e.preload_act_table_set("natural_log_exp_and_others"))
        ea = {}
        for b in range(NB):
            a = A[:, b * L:(b + 1) * L]
            ea[b] = sc.run(act(a, a, ACT.Exp, scale=la8), la)
        w4 = [t1[:, 0:512], t1[:, 512:1024], t2[:, 0:512], t2[:, 512:1024]]
        sr, hs = {}, {}
        for b in range(NB):
            a, w = A[:, b * L:(b + 1) * L], w4[b % 4]
            k = po.run(tt(w, a, a, ALU.mult), ea[b], hs.get(("w", b - 4)))
            k = ve.run(ts(w, w, 1.0, -1.0, ALU.min, ALU.mult), k)
            k = sc.run(act(w, w, ACT.Sqrt, bias=one), k)
            bb = B[:, b * L:(b + 1) * L]
            k = ve.run(tt(bb, bb, w, ALU.mult), k)
            hs["w", b] = k
            hs[b] = ve.run(lambda e, a=a, bb=bb: e.tensor_tensor_scan(a, a, bb, 0.0, ALU.mult, ALU.add), k)
        barrier()
        sc.put(lambda e: e.preload_act_table_set("natural_log_exp_and_others"))
        free = {}
        for b in range(NB):
            a, w, bk = A[:, b * L:(b + 1) * L], w4[b % 4], b % 4
            pe.wait(hs[b], free.get(b - 4))
            for t in range(TPB):
                k = pe.run(mm(ps[:, bk, t * 128:(t + 1) * 128], a[:, t * 128:(t + 1) * 128], wr[:, 2, :]))
            k = sc.run(act(w, ps[:, bk, :], ACT.Square), k, free.get(("w", b - 4)))
            r4 = rst[:, b * TPB:(b + 1) * TPB]
            k = ve.run(lambda e, w=w, r4=r4: e.tensor_reduce(r4, w.rearrange("p (t d) -> p t d", t=TPB), AX, ALU.add), k)
            free["w", b] = k
            k = sc.run(act(r4, r4, ACT.Ln, scale=1.0 / D, bias=eps_rms), k)
            k = sc.run(act(r4, r4, ACT.Exp, scale=-0.5), k)
            ve.wait(k, big)
            for t in range(TPB):
                k = ve.run(stt(a[:, t * 128:(t + 1) * 128], ps[:, bk, t * 128:(t + 1) * 128],
                               rst[:, b * TPB + t:b * TPB + t + 1], gam[:], ALU.mult, ALU.mult))
            free[b] = k
        barrier()

        vs_lo = [Dma(sem(f"s_vl{t}")) for t in range(TPB)]
        vs_hi = [Dma(sem(f"s_vh{t}")) for t in range(TPB)]
        for l in range(DEPTH):
            sc.put(lambda e: e.preload_act_table_set("natural_log_exp_and_others"))
            for i in range(2):
                for s in range(2):
                    k = ve.run(tt(tabl[:, i, :, s, :], tab[:, i, :, s, :],
                                  qks[:, i, l, s, :].unsqueeze(1).to_broadcast([128, TPB, DH]), ALU.mult), big)
            tabk = k
            T = {}

            def shift_in(b):
                x = X[:, b * L:(b + 1) * L]
                h = hT[:, b % 2, :]
                free = T.get(("qkv", 4 * b - 5))
                ve.run(cp(h[0:64, :], x[0:64, :]), free, T.get(("x", b)))
                T["h", b] = ve.run(cp(h[64:128, 1:L], x[64:128, 0:L - 1]))

            def turn_qk(i):
                c0 = t1[:]
                pe.wait(T["tn", i], T.get(("PT", i - 1)))
                for bank in (5, 6):
                    for c in range(4):
                        m = 4 * (bank - 5) + c
                        k = pe.run(tr(ps[:, bank, c * 128:(c + 1) * 128], c0[:, m * 128:(m + 1) * 128], idf[:]))
                    T["tp", i, bank] = k
                T["tqk", i] = k

            def keep_qk(i):
                t = i % TPB
                src = ps[:, 5, :].rearrange("p (g q) -> p g q", q=64)
                sc.run(act(qbd[0:64, :, 0:64], src[0:64], ACT.Copy), T["tp", i, 5], T.get(("sim", i - 1)))
                sc.run(act(qbd[64:128, :, 64:128], src[64:128], ACT.Copy))
                T["qk", i] = sc.run(act(kT[:, :, 64 + t * 128:64 + (t + 1) * 128],
                                        ps[:, 6, :].rearrange("p (c q) -> p c q", c=4), ACT.Copy), T["tp", i, 6])

            def qkv(i):
                b, t = divmod(i, TPB)
                h = hT[:, b % 2, t * 128:(t + 1) * 128]
                pe.wait(T["h", b], T.get(("t2", i - 1)), T.get(("v", i - 1)), big)
                for n in range(3):
                    k = pe.run(mm(ps[:, n, :], h, wqkv[:, l, n * 512:(n + 1) * 512]))
                T["qkv", i] = k

            def norm_qk(i):
                t = i % TPB
                qk = ps[:, 0:2, :].rearrange("p i (h e) -> p i h e", e=DH)
                s16 = ps[:, 0:2, :].rearrange("p i (h e) -> p (i h) e", e=DH)
                o1 = t1[:].rearrange("p (i h e) -> p i h e", i=2, e=DH)
                o2 = t2[:].rearrange("p (i h e) -> p i h e", i=2, e=DH)
                s2 = t2[:].rearrange("p (h e) -> p h e", e=DH)
                C = tabl[:, :, t, 0, :].unsqueeze(2).to_broadcast([128, 2, HEADS, DH])
                S = tabl[:, :, t, 1, :]
                k = sc.run(act(s2, s16, ACT.Square), T["qkv", i], T.get(("add", i - 1)))
                T["v", i] = sc.run(act(Vn[:, t, :], ps[:, 2, :], ACT.Copy), T.get(("av", i - 4)), T.get(("vs", i - 4)),
                                   T.get(("vslo", i - 3)))
                k = ve.run(lambda e: e.tensor_reduce(ss[:], s2, AX, ALU.add), k, T.get(("rr", i - 1)))
                T["ss", i] = ve.run(ts(ss[:], ss[:], 1e-24, None, ALU.max), k)
                ve.run(tt(o1, qk, C, ALU.mult), tabk, T.get(("tqk", i - 1)))
                for s in range(2):
                    k = ve.run(tt(o2[:, :, :, 32 * s:32 * s + 32], qk[:, :, :, 32 - 32 * s:64 - 32 * s],
                                  S[:, :, 32 * s:32 * s + 32].unsqueeze(2).to_broadcast([128, 2, HEADS, 32]), ALU.mult))
                T["t2", i] = k
                T["add", i] = po.run(tt(t1[:], t1[:], t2[:], ALU.add), k)

            def shift_v(i):
                t = i % TPB
                if t > 0:
                    T["vslo", i] = vs_lo[t].start(sp, Vs[0:64, t, :], Vn[64:128, t - 1, :], T["v", i], T.get(("av", i - 4)))
                T["vs", i] = vs_hi[t].start(sp, Vs[64:128, t, :], Vn[0:64, t, :], T["v", i], T.get(("av", i - 4)))

            def norm_rt(i):
                k = sc.run(act(rr[:], ss[:], ACT.Ln, scale=65536.0), T["ss", i], T.get(("tn", i - 1)))
                T["rr", i] = sc.run(act(rr[:], rr[:], ACT.Exp, scale=-0.5, bias=ln2x8), k)
                v = t1[:].rearrange("p (h e) -> p h e", e=DH)
                T["tn", i] = po.run(tt(v, v, rr[:].unsqueeze(2).to_broadcast([128, 16, DH]), ALU.mult),
                                    T["add", i], T["rr", i])

            def turn_p(i):
                pe.wait(T["pn", i], T["qk", i + 1] if ("qk", i + 1) in T else None)
                for g in range(8):
                    k = pe.run(tr(ps[:, 5 + g // 4, (g % 4) * 128:(g % 4 + 1) * 128], P[:, g, :], idf[:]))
                T["tp2", i] = k
                T["PT", i] = sc.run(act(PT[:], ps[:, 5:7, :].rearrange("p s (g q) -> p (s g) q", g=4), ACT.Copy),
                                    k, T.get(("av", i - 1)))

            def sims(i):
                t = i % TPB
                pe.wait(T["qk", i], T.get(("e", i - 1)))
                for s in range(2):
                    pe.put(mm(ps[:, 3 + s, :], idb[:], mask[:, min(t, 1), :], True, False))
                    for c in (2 * s, 2 * s + 1):
                        for w in range(2):
                            g = 2 * c + w
                            k0 = t * 128 + w * 64
                            k = pe.run(mm(ps[:, 3 + s, (g % 4) * 128:(g % 4 + 1) * 128], qbd[:, g, :],
                                          kT[:, c, k0:k0 + 128], False, True))
                T["sim", i] = k

            def softmax(i):
                S8 = ps[:, 3:5, :].rearrange("p s (g k) -> p (s g) k", g=4)
                k = ve.run(lambda e: e.tensor_reduce(nm[:], S8, AX, ALU.max, negate=True), T["sim", i], T.get(("e", i - 1)))
                sc.wait(k, T.get(("tp2", i - 1)), T.get(("pn", i - 1)))
                for g in range(8):
                    k = sc.run(act(P[:, g, :], ps[:, 3 + g // 4, (g % 4) * 128:(g % 4 + 1) * 128], ACT.Exp,
                                   bias=nm[:, g:g + 1], accum_out=den[:, g:g + 1]))
                T["e", i] = k
                k = ve.run(lambda e: e.reciprocal(rden[:], den[:]), k)
                T["pn", i] = ve.run(tt(P[:], P[:], rden[:].unsqueeze(2).to_broadcast([128, 8, 128]), ALU.mult), k)

            def attend(i):
                b, t = divmod(i, TPB)
                pe.wait(T["PT", i], T["v", i], T["vs", i], T.get(("vslo", i)), T.get(("o", i - 1)), T.get("misc"))
                for c in range(4):
                    for w in range(2):
                        for hh in range(2):
                            V = Vn if w else Vs
                            h = 2 * c + hh
                            k = pe.run(mm(ps[64 * hh:64 * hh + 64, 7, c * 128 + w * 64:c * 128 + w * 64 + 64],
                                          V[:, t, h * DH:(h + 1) * DH], PT[:, 2 * c + w, 64 * hh:64 * hh + 64]))
                T["av", i] = k
                T["o", i] = sc.run(act(oT[:, :, t * 128:(t + 1) * 128],
                                       ps[:, 7, :].rearrange("p (c q) -> p c q", c=4), ACT.Copy),
                                   k, T.get(("wo", b - 1)))

            def proj(b):
                pe.wait(T["o", 4 * b + 3])
                for c in range(4):
                    k = pe.run(mm(ps[:, 7, :], wo[:, l, c, :], oT[:, c, :], c == 0, c == 3))
                T["wo", b] = k
                x = X[:, b * L:(b + 1) * L]
                k = ve.run(tt(x, ps[:, 7, :], x, ALU.add), k)
                T["misc"] = k
                ve.run(cp(h2[0:64, :], x[0:64, :]), k, T.get(("hn", b - 1)))
                T["h2", b] = ve.run(cp(h2[64:128, 1:L], x[64:128, 0:L - 1]))

            def mean(b):
                k = pe.run(mm(ps[:, 7, :], avg[:], h2[:]), T["h2", b], T["o", min(4 * b + 4, NT - 1)])
                T["misc"] = T["hc", b] = ve.run(tt(sq[:], h2[:], ps[:, 7, :], ALU.subtract), k, T.get(("hn", b - 1)))
                T["sq", b] = sc.run(act(rsd[:], sq[:], ACT.Square), T["hc", b], T.get(("hn", b - 1)))

            def var(b):
                l9 = lcol(l, 0), lcol(l, 1)
                k = pe.run(mm(ps[:, 7, :], avg[:], rsd[:]), T["sq", b], T["o", min(4 * b + 5, NT - 1)])
                k = sc.run(act(rsd[:], ps[:, 7, :], ACT.Ln, bias=eps_ln), k)
                T["misc"] = k
                k = sc.run(act(rsd[:], rsd[:], ACT.Exp, scale=-0.5), k)
                hn = B[:, b * L:(b + 1) * L]
                k = ve.run(tt(hn, sq[:], rsd[:], ALU.mult), k)
                T["hn", b] = ve.run(ts(hn, hn, l9[0], l9[1], ALU.mult, ALU.add), k)

            shift_in(0)
            for i in range(NT + 6):
                if 1 <= i <= NT:
                    turn_qk(i - 1)
                    keep_qk(i - 1)
                if i >= 6 and (i - 6) % 4 == 0:
                    proj((i - 6) // 4)
                if i >= 7 and (i - 7) % 4 == 0:
                    mean((i - 7) // 4)
                if i >= 8 and (i - 8) % 4 == 0:
                    var((i - 8) // 4)
                if i < NT:
                    qkv(i)
                    norm_qk(i)
                    shift_v(i)
                    if i % TPB == 2 and i // TPB + 1 < NB:
                        shift_in(i // TPB + 1)
                if 2 <= i < NT + 2:
                    turn_p(i - 2)
                if i < NT:
                    norm_rt(i)
                if 1 <= i <= NT:
                    sims(i - 1)
                    softmax(i - 1)
                if 2 <= i < NT + 2:
                    attend(i - 2)
            for b in range((NT + 6 - 7) // 4 + 1, NB):
                mean(b)
            for b in range((NT + 6 - 8 - 1) // 4 + 1, NB):
                var(b)
            barrier()

            gl = [t1[:, 0:512], t1[:, 512:1024], t2[:, 0:512]]
            hh = [P[:].rearrange("p g q -> p (g q)"), PT[:].rearrange("p g q -> p (g q)")]
            hx = [[hh[0][:, 0:512], hh[0][:, 512:1024], t2[:, 512:1024]],
                  [hh[1][:, 0:512], hh[1][:, 512:1024], rsd[:]]]
            U = {}
            for b in range(NB + 1):
                if b < NB:
                    hn = B[:, b * L:(b + 1) * L]
                    for j, (o, n) in enumerate(CH):
                        kg = pe.run(mm(ps[0:n, 3 + j, :], w1[:, l, HID + o:HID + o + n], hn), U.get(("g", j)))
                        ka = pe.run(mm(ps[0:n, j, :], w1[:, l, o:o + n], hn), U.get(("a", j)))
                        U["g", j] = sc.run(act(gl[j][0:n, :], ps[0:n, 3 + j, :], ACT.Gelu,
                                               bias=lcol(l, 6 + j)[0:n, :]), kg, U.get(("a", j)))
                        U["a", j] = ve.run(stt(hx[b % 2][j][0:n, :], ps[0:n, j, :], lcol(l, 3 + j)[0:n, :],
                                               gl[j][0:n, :], ALU.add, ALU.mult), ka, U["g", j], U.get(("y", b - 2)))
                        U["h", b] = U["a", j]
                if b >= 1:
                    c = b - 1
                    pe.wait(U["h", c], U.get(("x", c - 2)))
                    for j, (o, n) in enumerate(CH):
                        k = pe.run(mm(ps[:, 6 + c % 2, :], w2[0:n, l, j, :], hx[c % 2][j][0:n, :], j == 0, j == 2))
                    U["y", c] = k
                    x = X[:, c * L:(c + 1) * L]
                    U["x", c] = ve.run(stt(x, ps[:, 6 + c % 2, :], lcol(l, 2), x, ALU.add, ALU.add), k)
            barrier()

        st_out = [Dma(sem(f"s_o{i}")) for i in range(4)]
        last, fr, ot = {}, {}, {}
        for b in range(4):
            xtok[b] = load_x(b)
        gs = [P[:].rearrange("p g q -> p (g q)")[:, 0:512], P[:].rearrange("p g q -> p (g q)")[:, 512:1024],
              PT[:].rearrange("p g q -> p (g q)")[:, 0:512], PT[:].rearrange("p g q -> p (g q)")[:, 512:1024]]
        for b in range(NB):
            x, s, g, bk = X[:, b * L:(b + 1) * L], A[:, b * L:(b + 1) * L], gs[b % 4], b % 4
            pe.wait(fr.get(b - 4))
            for t in range(TPB):
                k = pe.run(tr(ps[:, bk, t * 128:(t + 1) * 128], x[:, t * 128:(t + 1) * 128], idf[:]))
            fr[b] = k = sc.run(act(g, ps[:, bk, :], ACT.Silu), k, ot.get(b - 4))
            k = ve.run(tt(g, g, s, ALU.mult), k)
            k = ve.run(tt(g, g, xt[b % 4], ALU.add), k, xtok[b])
            ot[b] = st_out[bk].start(sp, od[b], g.rearrange("p (t d) -> p t d", t=TPB), k)
            last[bk] = ot[b]
            if b + 4 < NB:
                xtok[b + 4] = load_x(b + 4, k)
        sp.wait(*last.values())

        block = ctx.enter_context(nc.Block())

        @block.tensor
        def _(e):
            pe.emit(e)

        @block.scalar
        def _(e):
            sc.emit(e)

        @block.vector
        def _(e):
            ve.emit(e)

        @block.gpsimd
        def _(e):
            po.emit(e)

        @block.sync
        def _(e):
            sp.emit(e)


def constants():
    f = np.float32
    half = np.arange(0, DH, 2, dtype=f)
    inv = (f(1.0) / np.power(f(10000.0), half / f(DH), dtype=f)).astype(f)
    t = np.arange(L, dtype=f)
    fr = (t[:, None] * inv[None, :]).astype(f)
    fr = np.concatenate([fr, fr], -1).astype(np.float64)
    base = (half + f(0.4 * DH)) / f(1.4 * DH)
    power = (t - f(L // 2)) / f(WIN // 2)
    scale = np.power(base[None, :].astype(np.float64), power[:, None].astype(np.float64))
    scale = np.concatenate([scale, scale], -1)
    cos, sin = np.cos(fr), np.sin(fr)
    sgn = np.concatenate([-np.ones(32), np.ones(32)])[None, :]
    tab = np.stack([np.stack([8 * cos * scale, 8 * sin * scale * sgn], 1),
                    np.stack([cos / scale, sin / scale * sgn], 1)], 0)
    tab = tab.reshape(2, TPB, 128, 2, DH).transpose(2, 0, 1, 3, 4).astype(f)
    q = np.arange(64)[:, None]
    k = np.arange(128)[None, :]
    ok = (k >= q) & (k <= q + 64)
    first = ok & (k >= 64)
    mask = np.zeros((2, 2, 64, 2, 2, 128), f)
    for v in range(2):
        for w in range(2):
            good = first if (v == 0 and w == 0) else ok
            mask[v, :, :, :, w, :] = np.where(good, 0.0, -1e30)[None, :, None, :]
    mask = mask.reshape(2, 128, 512).transpose(1, 0, 2)
    eye = np.eye(128, dtype=f)
    return tab, mask, eye


def kernel(**inputs):
    import ml_dtypes
    import concourse.bacc as bacc
    from concourse.bass_utils import run_bass_kernel_spmd as run

    a = {n.split("_", 2)[2]: np.ascontiguousarray(v) for n, v in inputs.items()}
    tab, mask, eye = constants()
    cols = np.zeros((128, 32), np.float32)
    cols[:, 0], cols[:, 1], cols[:, 2], cols[:, 3] = a["conv_b"], a["b_r"], a["b_i"], a["log_a"]
    cols[:, 4:8] = a["conv_w"][:, 0, :]
    w2 = np.zeros((128, DEPTH, 3, 128), np.float32)
    for l in range(DEPTH):
        c = cols[:, 8 + 9 * l:17 + 9 * l]
        c[:, 0], c[:, 1], c[:, 2] = a["ln_g"][l], a["ln_b"][l], a["b2"][l]
        for j, (o, n) in enumerate(CH):
            c[:n, 3 + j] = a["b1"][l, o:o + n]
            c[:n, 6 + j] = a["b1"][l, HID + o:HID + o + n]
            w2[:n, l, j, :] = a["w2"][l, o:o + n, :]
    feed = {
        "x": a["x"], "cols": cols, "idf": eye, "idb": eye.astype(ml_dtypes.bfloat16),
        "mask": mask.astype(ml_dtypes.bfloat16), "avg": np.full((128, 128), 1.0 / D, np.float32), "tab": tab,
        "wr": np.stack([a["W_r"].T, a["W_i"].T, a["W_out"].T], 1),
        "wqkv": a["wqkv"].transpose(1, 0, 2), "w1": a["w1"].transpose(1, 0, 2), "w2": w2,
        "wo": a["wo"].reshape(DEPTH, 4, 128, 128).transpose(2, 0, 1, 3),
        "gamma": a["gamma"], "q_scale": a["q_scale"], "k_scale": a["k_scale"],
    }
    feed = {n: np.ascontiguousarray(v) for n, v in feed.items()}
    nc = bacc.Bacc("TRN2", target_bir_lowering=False, num_devices=1)
    d = {n: nc.dram_tensor(f"in_{n}", v.shape, mybir.dt.from_np(v.dtype), kind="ExternalInput").ap() for n, v in feed.items()}
    out = nc.dram_tensor("out_0", (NB, L, D), F32, kind="ExternalOutput").ap()
    program(nc, d, out)
    r = run(nc, [{f"in_{n}": v for n, v in feed.items()}], core_ids=[0])
    return r.results[0]["out_0"]
```

```python
from contextlib import ExitStack

import numpy as np

import concourse.bass as bass
from concourse import mybir

F32 = mybir.dt.float32
BF16 = mybir.dt.bfloat16
ALU = mybir.AluOpType
ACT = mybir.ActivationFunctionType
AX = mybir.AxisListType.X

NB, L, D = 16, 512, 128
TPB = L // 128
NT = NB * TPB
DEPTH, HEADS, DH, WIN = 2, 8, 64, 64
INNER = HEADS * DH
HID = 341
CH = [(0, 128), (128, 128), (256, 85)]
LN_EPS = 1e-5
RMS_EPS = 1e-6
LN2 = 0.6931471805599453


class Queue:

    def __init__(self, sem):
        self.sem, self.items, self.count, self.seen, self.last = sem, [], 0, {}, None

    def wait(self, *toks):
        for t in toks:
            if t is not None and self.seen.get(id(t[0]), 0) < t[1]:
                self.seen[id(t[0])] = t[1]
                self.items.append(lambda e, t=t: e.wait_ge(t[0], t[1]))

    def put(self, ins):
        self.items.append(ins)

    def run(self, ins, *waits):
        self.wait(*waits)
        self.count += 1
        self.last = (self.sem, self.count)
        self.items.append(lambda e: ins(e).then_inc(self.sem, 1))
        return self.last

    def emit(self, e):
        for i in self.items:
            i(e)


class Dma:

    def __init__(self, sem):
        self.sem, self.count = sem, 0

    def start(self, q, out, in_, *waits):
        q.wait(*waits)
        self.count += 16
        q.put(lambda e: e.dma_start(out, in_).then_inc(self.sem, 16))
        return (self.sem, self.count)


def mm(out, lhsT, rhs, start=True, stop=True):
    return lambda e: e.matmul(out, lhsT, rhs, start=start, stop=stop, skip_group_check=True)


def tr(out, in_, ident):
    return lambda e: e.transpose(out, in_, ident)


def act(out, in_, f, **kw):
    return lambda e: e.activation(out, in_, f, **kw)


def tt(out, a, b, op):
    return lambda e: e.tensor_tensor(out, a, b, op)


def ts(out, a, s1, s2, op0, op1=None):
    if op1 is None:
        return lambda e: e.tensor_scalar(out, a, s1, None, op0)
    return lambda e: e.tensor_scalar(out, a, s1, s2, op0, op1)


def stt(out, a, s, b, op0, op1):
    return lambda e: e.scalar_tensor_tensor(out, a, s, b, op0, op1)


def cp(out, a):
    return lambda e: e.tensor_copy(out, a)


def zero(out, v=0.0):
    return lambda e: e.memset(out, v)


def program(nc, d, out):
    ctx = ExitStack()
    with ctx:
        def sb(name, shape, dt=F32):
            return ctx.enter_context(nc.sbuf_tensor(name, shape, dt))

        def sem(name):
            return ctx.enter_context(nc.semaphore(name))

        pe, sc, ve, po, sp = (Queue(sem(n)) for n in ("s_pe", "s_act", "s_dve", "s_pool", "s_sp"))

        X = sb("X", [128, NB * L])
        A = sb("A", [128, NB * L])
        B = sb("B", [128, NB * L])
        wqkv = sb("wqkv", [128, DEPTH, 3 * INNER])
        wo = sb("wo", [128, DEPTH, 4, 128])
        w1 = sb("w1", [128, DEPTH, 2 * HID])
        w2 = sb("w2", [128, DEPTH, 3, 128])
        wr = sb("wr", [128, 3, 128])
        tabl = sb("tabl", [128, 2, TPB, 2, DH])
        qks = sb("qks", [128, 2, DEPTH, 2, DH])
        cols = sb("cols", [128, 32])
        gam = sb("gam", [128, 128])
        idf = sb("idf", [128, 128])
        idb = sb("idb", [128, 128], BF16)
        avg = sb("avg", [128, 128])
        mask = sb("mask", [128, 2, 512], BF16)
        cst = sb("cst", [128, 8])
        ab = sb("ab", [128, 16])
        st = sb("st", [128, 4, 6])
        mv = sb("mv", [128, NT, 2])
        rst = sb("rst", [128, NT])
        ss = sb("ss", [128, 16])
        rr = sb("rr", [128, 16])
        nm = sb("nm", [128, 8])
        den = sb("den", [128, 8])
        rden = sb("rden", [128, 8])
        t1 = sb("t1", [128, 1024])
        t3 = sb("t3", [128, 1024])
        t2 = sb("t2", [128, 1024])
        P = sb("P", [128, 8, 128])
        PT = sb("PT", [128, 8, 128])
        qbd = sb("qbd", [128, 8, 128])
        kT = sb("kT", [128, 4, 64 + L])
        Vn = sb("Vn", [128, TPB, INNER])
        Vs = sb("Vs", [128, TPB, INNER])
        oT = sb("oT", [128, 4, L])
        hT = sb("hT", [128, 2, L])
        h2 = sb("h2", [128, L])
        sq = sb("sq", [128, L])
        rsd = sb("rsd", [128, L])
        ps = ctx.enter_context(nc.psum_tensor("ps", [128, 8, 512], F32))

        CB, BR, BI, LA, CW = (cols[:, i:i + 1] for i in range(5))
        cw = [cols[:, 4 + j:5 + j] for j in range(4)]

        def lcol(l, j):
            return cols[:, 8 + 9 * l + j:9 + 9 * l + j]

        one, eps_ln, eps_rms, ln2x8 = (cst[:, i:i + 1] for i in range(4))

        ld = Dma(sem("s_ld"))
        lw = Dma(sem("s_lw"))
        lt = Dma(sem("s_tab"))
        ring = [Dma(sem(f"s_x{i}")) for i in range(4)]
        xt = [t1[:, 0:512], t1[:, 512:1024], t2[:, 0:512], t2[:, 512:1024]]
        xd = d["x"].rearrange("b (t p) d -> b p t d", p=128)
        od = out.rearrange("b (t p) d -> b p t d", p=128)

        def load_x(b, *waits):
            return ring[b % 4].start(sp, xt[b % 4].rearrange("p (t d) -> p t d", t=TPB), xd[b], *waits)

        xtok = {}
        for b in range(4):
            xtok[b] = load_x(b)
        for t_, n in ((cols, "cols"), (idf, "idf"), (wr, "wr")):
            small = ld.start(sp, t_[:], d[n])
        for t_, n in ((wqkv, "wqkv"), (idb, "idb"), (mask, "mask"), (avg, "avg"), (wo, "wo"),
                      (w1, "w1"), (w2, "w2")):
            big = lw.start(sp, t_[:], d[n])
        big = lw.start(sp, gam[:], d["gamma"].partition_broadcast(128))
        for i, n in enumerate(("q_scale", "k_scale")):
            flat = d[n].rearrange("l e -> (l e)")
            big = lw.start(sp, qks[:, i, :, 0, :], d[n].partition_broadcast(128))
            big = lw.start(sp, qks[:, i, :, 1, 0:32], d[n][:, 32:64].partition_broadcast(128))
            big = lw.start(sp, qks[:, i, :, 1, 32:64], d[n][:, 0:32].partition_broadcast(128))

        for i, v in enumerate((1.0, LN_EPS, RMS_EPS, 8 * LN2)):
            ve.run(zero(cst[:, i:i + 1], v))
        ve.run(zero(qbd[:]))
        ve.run(zero(kT[:, :, 0:64]))
        ve.run(zero(Vs[0:64, 0, :]))
        ve.run(zero(hT[64:128, :, 0:1]))
        consts = ve.run(zero(h2[64:128, 0:1]))

        def barrier():
            toks = [q.last for q in (pe, sc, ve, po) if q.last]
            for q in (pe, sc, ve, po, sp):
                q.wait(*toks)

        sc.put(lambda e: e.preload_act_table_set("natural_log_exp_and_others"))
        sc.wait(consts)
        xn = [A[:, 0:512], A[:, 512:1024]]
        xn_free = {}
        for b in range(NB):
            xb = xt[b % 4].rearrange("p (t d) -> p t d", t=TPB)
            ve.wait(xtok[b])
            for t in range(TPB):
                k = ve.run(lambda e, t=t, xb=xb: e.bn_stats(st[:, t, :], xb[:, t, :]))
            ve.wait(k)
            for t in range(TPB):
                k = ve.run(lambda e, t=t, b=b: e.bn_aggr(mv[:, b * TPB + t, :], st[:, t, :]))
            r4 = rst[:, b * TPB:(b + 1) * TPB]
            k = sc.run(act(r4, mv[:, b * TPB:(b + 1) * TPB, 1], ACT.Ln, bias=eps_ln), k)
            k = sc.run(act(r4, r4, ACT.Exp, scale=-0.5), k)
            ve.wait(k, xn_free.get(b - 2))
            for t in range(TPB):
                n = b * TPB + t
                k = ve.run(ts(xn[b % 2][:, t * 128:(t + 1) * 128], xb[:, t, :], mv[:, n, 0:1], rst[:, n:n + 1],
                              ALU.subtract, ALU.mult))
            if b + 4 < NB:
                xtok[b + 4] = load_x(b + 4, k)
            pe.wait(k, small, xn_free.get(("ps", b - 2)))
            for t in range(TPB):
                k = pe.run(tr(ps[:, b % 2, t * 128:(t + 1) * 128], xn[b % 2][:, t * 128:(t + 1) * 128], idf[:]))
            xn_free[b] = k
            xn_free["ps", b] = sc.run(act(X[:, b * L:(b + 1) * L], ps[:, b % 2, :], ACT.Copy), k)
        barrier()

        ax, ez, u, dd, lnu, ru, la8 = (ab[:, i:i + 1] for i in range(7))
        nx, mx = ab[:, 7:8], ab[:, 8:9]
        k = ve.run(ts(nx, LA, -1.0, None, ALU.mult), small)
        k = ve.run(tt(ax, LA, nx, ALU.max), k)
        k = sc.run(act(ez, ax, ACT.Exp, scale=-1.0), k)
        k = ve.run(ts(u, ez, 1.0, None, ALU.add), k)
        k2 = sc.run(act(lnu, u, ACT.Ln), k)
        k = ve.run(ts(dd, u, -1.0, None, ALU.add), k)
        k = ve.run(tt(dd, ez, dd, ALU.subtract), k)
        ve.run(ts(mx, nx, 0.0, None, ALU.max))
        k = ve.run(lambda e: e.reciprocal(ru, u), k)
        k = ve.run(stt(dd, dd, ru, lnu, ALU.mult, ALU.add), k, k2)
        k = ve.run(tt(dd, dd, mx, ALU.add), k)
        la = ve.run(ts(la8, dd, -8.0, None, ALU.mult), k)

        xc = [t1[:, 0:512], t1[:, 512:1024]]
        it = [t2[:, 0:512], t2[:, 512:1024]]
        free = {}
        for b in range(NB):
            x = X[:, b * L:(b + 1) * L]
            y = xc[b % 2]
            k = ve.run(ts(y, x, cw[3], CB, ALU.mult, ALU.add), free.get(("pe", b - 2)))
            for s in (1, 2, 3):
                k = ve.run(stt(y[:, s:], x[:, :L - s], cw[3 - s], y[:, s:], ALU.mult, ALU.add), k)
            p0, p1 = 2 * (b % 2), 2 * (b % 2) + 1
            k1 = pe.run(mm(ps[:, p0, :], wr[:, 0, :], y), k, free.get(("r", b - 2)))
            k2 = pe.run(mm(ps[:, p1, :], wr[:, 1, :], y), free.get(("i", b - 2)))
            free["pe", b] = k2
            free["r", b] = sc.run(act(A[:, b * L:(b + 1) * L], ps[:, p0, :], ACT.Sigmoid, bias=BR), k1)
            k = sc.run(act(it[b % 2], ps[:, p1, :], ACT.Sigmoid, bias=BI), k2, free.get(("dv", b - 2)))
            free["i", b] = k
            free["dv", b] = ve.run(tt(B[:, b * L:(b + 1) * L], it[b % 2], y, ALU.mult), k)
        barrier()
        sc.put(lambda e: e.preload_act_table_set("natural_log_exp_and_others"))
        ea = {}
        for b in range(NB):
            a = A[:, b * L:(b + 1) * L]
            ea[b] = sc.run(act(a, a, ACT.Exp, scale=la8), la)
        w4 = [t1[:, 0:512], t1[:, 512:1024], t2[:, 0:512], t2[:, 512:1024]]
        sr, hs = {}, {}
        for b in range(NB):
            a, w = A[:, b * L:(b + 1) * L], w4[b % 4]
            k = po.run(tt(w, a, a, ALU.mult), ea[b], hs.get(("w", b - 4)))
            k = ve.run(ts(w, w, 1.0, -1.0, ALU.min, ALU.mult), k)
            k = sc.run(act(w, w, ACT.Sqrt, bias=one), k)
            bb = B[:, b * L:(b + 1) * L]
            k = ve.run(tt(bb, bb, w, ALU.mult), k)
            hs["w", b] = k
            hs[b] = ve.run(lambda e, a=a, bb=bb: e.tensor_tensor_scan(a, a, bb, 0.0, ALU.mult, ALU.add), k)
        barrier()
        sc.put(lambda e: e.preload_act_table_set("natural_log_exp_and_others"))
        free = {}
        for b in range(NB):
            a, w, bk = A[:, b * L:(b + 1) * L], w4[b % 4], b % 4
            pe.wait(hs[b], free.get(b - 4))
            for t in range(TPB):
                k = pe.run(mm(ps[:, bk, t * 128:(t + 1) * 128], a[:, t * 128:(t + 1) * 128], wr[:, 2, :]))
            k = sc.run(act(w, ps[:, bk, :], ACT.Square), k, free.get(("w", b - 4)))
            r4 = rst[:, b * TPB:(b + 1) * TPB]
            k = ve.run(lambda e, w=w, r4=r4: e.tensor_reduce(r4, w.rearrange("p (t d) -> p t d", t=TPB), AX, ALU.add), k)
            free["w", b] = k
            k = sc.run(act(r4, r4, ACT.Ln, scale=1.0 / D, bias=eps_rms), k)
            k = sc.run(act(r4, r4, ACT.Exp, scale=-0.5), k)
            ve.wait(k, big)
            for t in range(TPB):
                k = ve.run(stt(a[:, t * 128:(t + 1) * 128], ps[:, bk, t * 128:(t + 1) * 128],
                               rst[:, b * TPB + t:b * TPB + t + 1], gam[:], ALU.mult, ALU.mult))
            free[b] = k
        barrier()

        vs_lo = [Dma(sem(f"s_vl{t}")) for t in range(TPB)]
        vs_hi = [Dma(sem(f"s_vh{t}")) for t in range(TPB)]
        for l in range(DEPTH):
            sc.put(lambda e: e.preload_act_table_set("natural_log_exp_and_others"))
            tb = lt.start(sp, tabl[:], d["tab"])
            for i in range(2):
                for s in range(2):
                    k = ve.run(tt(tabl[:, i, :, s, :], tabl[:, i, :, s, :],
                                  qks[:, i, l, s, :].unsqueeze(1).to_broadcast([128, TPB, DH]), ALU.mult), big, tb)
            tabk = k
            T = {}
            tq = [t1, t3]

            def vbank(i):
                return 2 if i % 2 else 7

            def obank(i):
                return vbank(i + 4)


            def shift_in(b):
                x = X[:, b * L:(b + 1) * L]
                h = hT[:, b % 2, :]
                free = T.get(("vm", 4 * b - 5))
                ve.run(cp(h[0:64, :], x[0:64, :]), free, T.get(("x", b)))
                T["h", b] = ve.run(cp(h[64:128, 1:L], x[64:128, 0:L - 1]))

            def turn_qk(i):
                c0 = tq[i % 2][:]
                pe.wait(T["tn", i], T.get(("PT", i - 1)))
                for bank in (5, 6):
                    for c in range(4):
                        m = 4 * (bank - 5) + c
                        k = pe.run(tr(ps[:, bank, c * 128:(c + 1) * 128], c0[:, m * 128:(m + 1) * 128], idf[:]))
                    T["tp", i, bank] = k
                T["tqk", i] = k

            def keep_qk(i):
                t = i % TPB
                src = ps[:, 5, :].rearrange("p (g q) -> p g q", q=64)
                sc.run(act(qbd[0:64, :, 0:64], src[0:64], ACT.Copy), T["tp", i, 5], T.get(("sim", i - 1)))
                T["qk", i] = sc.run(act(qbd[64:128, :, 64:128], src[64:128], ACT.Copy))
                T["kt", i] = ve.run(cp(kT[:, :, 64 + t * 128:64 + (t + 1) * 128],
                                       ps[:, 6, :].rearrange("p (c q) -> p c q", c=4)), T["tp", i, 6],
                                    T.get(("sim", i - 1)))

            def qk_proj(i):
                b, t = divmod(i, TPB)
                h = hT[:, b % 2, t * 128:(t + 1) * 128]
                pe.wait(T["h", b], T.get(("t2", i - 1)), big)
                for n in range(2):
                    k = pe.run(mm(ps[:, n, :], h, wqkv[:, l, n * 512:(n + 1) * 512]))
                T["qkv", i] = k

            def square(i):
                s2 = t2[:].rearrange("p (h e) -> p h e", e=DH)
                s16 = ps[:, 0:2, :].rearrange("p i (h e) -> p (i h) e", e=DH)
                k = sc.run(act(s2, s16, ACT.Square), T["qkv", i], T.get(("add", i - 1)))
                k = ve.run(lambda e: e.tensor_reduce(ss[:], s2, AX, ALU.add), k, T.get(("rr", i - 1)))
                T["ss", i] = ve.run(ts(ss[:], ss[:], 1e-24, None, ALU.max), k)

            def rotate(i):
                t = i % TPB
                r1 = tq[i % 2]
                qk = ps[:, 0:2, :].rearrange("p i (h e) -> p i h e", e=DH)
                o1 = r1[:].rearrange("p (i h e) -> p i h e", i=2, e=DH)
                o2 = t2[:].rearrange("p (i h e) -> p i h e", i=2, e=DH)
                C = tabl[:, :, t, 0, :].unsqueeze(2).to_broadcast([128, 2, HEADS, DH])
                S = tabl[:, :, t, 1, :]
                ve.run(tt(o1, qk, C, ALU.mult), tabk, T.get(("tqk", i - 2)))
                for s in range(2):
                    k = ve.run(tt(o2[:, :, :, 32 * s:32 * s + 32], qk[:, :, :, 32 - 32 * s:64 - 32 * s],
                                  S[:, :, 32 * s:32 * s + 32].unsqueeze(2).to_broadcast([128, 2, HEADS, 32]), ALU.mult))
                T["t2", i] = k
                T["add", i] = po.run(tt(r1[:], r1[:], t2[:], ALU.add), k)

            def v_proj(i):
                b, t = divmod(i, TPB)
                h = hT[:, b % 2, t * 128:(t + 1) * 128]
                pe.wait(T["h", b], T.get(("v", i - 1)), T.get(("o", i - 4)))
                T["vm", i] = pe.run(mm(ps[:, vbank(i), :], h, wqkv[:, l, 1024:1536]))

            def keep_v(i):
                t = i % TPB
                T["v", i] = sc.run(act(Vn[:, t, :], ps[:, vbank(i), :], ACT.Copy), T["vm", i], T.get(("av", i - 4)),
                                   T.get(("vs", i - 4)), T.get(("vslo", i - 3)))
                shift_v(i)

            def shift_v(i):
                t = i % TPB
                if t > 0:
                    T["vslo", i] = vs_lo[t].start(sp, Vs[0:64, t, :], Vn[64:128, t - 1, :], T["v", i], T.get(("av", i - 4)))
                T["vs", i] = vs_hi[t].start(sp, Vs[64:128, t, :], Vn[0:64, t, :], T["v", i], T.get(("av", i - 4)))

            def norm_rt(i):
                k = sc.run(act(rr[:], ss[:], ACT.Ln, scale=65536.0), T["ss", i], T.get(("tn", i - 1)))
                T["rr", i] = sc.run(act(rr[:], rr[:], ACT.Exp, scale=-0.5, bias=ln2x8), k)

            def scale_qk(i):
                v = tq[i % 2][:].rearrange("p (h e) -> p h e", e=DH)
                T["tn", i] = po.run(tt(v, v, rr[:].unsqueeze(2).to_broadcast([128, 16, DH]), ALU.mult),
                                    T["add", i], T["rr", i])

            def turn_p(i):
                pe.wait(T["pn", i], T.get(("qk", i + 1)), T.get(("kt", i + 1)))
                for g in range(8):
                    k = pe.run(tr(ps[:, 5 + g // 4, (g % 4) * 128:(g % 4 + 1) * 128], P[:, g, :], idf[:]))
                T["tp2", i] = k

            def keep_p(i):
                T["PT", i] = sc.run(act(PT[:], ps[:, 5:7, :].rearrange("p s (g q) -> p (s g) q", g=4), ACT.Copy),
                                    T["tp2", i], T.get(("av", i - 1)))

            def sims(i):
                t = i % TPB
                pe.wait(T["qk", i], T["kt", i], T.get(("e", i - 1)))
                for s in range(2):
                    pe.put(mm(ps[:, 3 + s, :], idb[:], mask[:, min(t, 1), :], True, False))
                    for c in (2 * s, 2 * s + 1):
                        for w in range(2):
                            g = 2 * c + w
                            k0 = t * 128 + w * 64
                            k = pe.run(mm(ps[:, 3 + s, (g % 4) * 128:(g % 4 + 1) * 128], qbd[:, g, :],
                                          kT[:, c, k0:k0 + 128], False, True))
                T["sim", i] = k

            def row_max(i):
                S8 = ps[:, 3:5, :].rearrange("p s (g k) -> p (s g) k", g=4)
                T["nm", i] = ve.run(lambda e: e.tensor_reduce(nm[:], S8, AX, ALU.max, negate=True),
                                    T["sim", i], T.get(("e", i - 1)))

            def exps(i):
                sc.wait(T["nm", i], T.get(("tp2", i - 1)), T.get(("pn", i - 1)))
                for g in range(8):
                    k = sc.run(act(P[:, g, :], ps[:, 3 + g // 4, (g % 4) * 128:(g % 4 + 1) * 128], ACT.Exp,
                                   bias=nm[:, g:g + 1], accum_out=den[:, g:g + 1]))
                T["e", i] = k

            def normalise(i):
                k = ve.run(lambda e: e.reciprocal(rden[:], den[:]), T["e", i])
                T["pn", i] = ve.run(tt(P[:], P[:], rden[:].unsqueeze(2).to_broadcast([128, 8, 128]), ALU.mult), k)

            def attend(i):
                b, t = divmod(i, TPB)
                pe.wait(T["PT", i], T["v", i], T["vs", i], T.get(("vslo", i)), T.get(("o", i - 1)), T.get(("v", i + 2)), T.get("misc"))
                for c in range(4):
                    for w in range(2):
                        for hh in range(2):
                            V = Vn if w else Vs
                            h = 2 * c + hh
                            k = pe.run(mm(ps[64 * hh:64 * hh + 64, obank(i), c * 128 + w * 64:c * 128 + w * 64 + 64],
                                          V[:, t, h * DH:(h + 1) * DH], PT[:, 2 * c + w, 64 * hh:64 * hh + 64]))
                T["av", i] = k

            def keep_o(i):
                b, t = divmod(i, TPB)
                T["o", i] = sc.run(act(oT[:, :, t * 128:(t + 1) * 128],
                                       ps[:, obank(i), :].rearrange("p (c q) -> p c q", c=4), ACT.Copy),
                                   T["av", i], T.get(("wo", b - 1)))

            def proj(b, z):
                pe.wait(T["o", 4 * b + 3], T.get(("v", min(z + 2, NT - 1))))
                for c in range(4):
                    k = pe.run(mm(ps[:, obank(z), :], wo[:, l, c, :], oT[:, c, :], c == 0, c == 3))
                T["wo", b] = k
                x = X[:, b * L:(b + 1) * L]
                k = ve.run(tt(x, ps[:, obank(z), :], x, ALU.add), k)
                T["misc"] = k
                ve.run(cp(h2[0:64, :], x[0:64, :]), k, T.get(("hn", b - 1)))
                T["h2", b] = ve.run(cp(h2[64:128, 1:L], x[64:128, 0:L - 1]))

            def mean(b, z):
                k = pe.run(mm(ps[:, obank(z), :], avg[:], h2[:]), T["h2", b], T.get(("v", min(z + 2, NT - 1))),
                           T.get(("o", min(z - 2, NT - 1))))
                T["misc"] = T["hc", b] = ve.run(tt(sq[:], h2[:], ps[:, obank(z), :], ALU.subtract), k, T.get(("hn", b - 1)))
                T["sq", b] = sc.run(act(rsd[:], sq[:], ACT.Square), T["hc", b], T.get(("hn", b - 1)))

            def var(b, z):
                l9 = lcol(l, 0), lcol(l, 1)
                k = pe.run(mm(ps[:, obank(z), :], avg[:], rsd[:]), T["sq", b], T.get(("v", min(z + 2, NT - 1))),
                           T.get(("o", min(z - 2, NT - 1))), T["misc"])
                k = sc.run(act(rsd[:], ps[:, obank(z), :], ACT.Ln, bias=eps_ln), k)
                T["misc"] = k
                k = sc.run(act(rsd[:], rsd[:], ACT.Exp, scale=-0.5), k)
                hn = B[:, b * L:(b + 1) * L]
                k = ve.run(tt(hn, sq[:], rsd[:], ALU.mult), k)
                T["hn", b] = ve.run(ts(hn, hn, l9[0], l9[1], ALU.mult, ALU.add), k)

            shift_in(0)
            for i in range(NT + 9):
                j, n = i - 2, i - 3
                if 0 <= j < NT:
                    turn_qk(j)
                    keep_qk(j)
                if 0 <= n < NT:
                    normalise(n)
                if 0 <= i - 1 < NT:
                    keep_v(i - 1)
                if 0 <= n - 1 < NT:
                    keep_o(n - 1)
                if i < NT:
                    qk_proj(i)
                    square(i)
                    norm_rt(i)
                    if i % TPB == 2 and i // TPB + 1 < NB:
                        shift_in(i // TPB + 1)
                if i >= 7 and (i - 7) % 4 == 0 and (i - 7) // 4 < NB:
                    proj((i - 7) // 4, n)
                if i >= 8 and (i - 8) % 4 == 0 and (i - 8) // 4 < NB:
                    mean((i - 8) // 4, n)
                if i >= 9 and (i - 9) % 4 == 0 and (i - 9) // 4 < NB:
                    var((i - 9) // 4, n)
                if 0 <= j < NT:
                    sims(j)
                    row_max(j)
                if i < NT:
                    rotate(i)
                    scale_qk(i)
                if 0 <= n < NT:
                    turn_p(n)
                    keep_p(n)
                if 0 <= j < NT:
                    exps(j)
                if i < NT:
                    v_proj(i)
                if 0 <= n < NT:
                    attend(n)
            barrier()

            gl = [t1[:, 0:512], t1[:, 512:1024], t2[:, 0:512]]
            hh = [P[:].rearrange("p g q -> p (g q)"), PT[:].rearrange("p g q -> p (g q)")]
            hx = [[hh[0][:, 0:512], hh[0][:, 512:1024], t2[:, 512:1024]],
                  [hh[1][:, 0:512], hh[1][:, 512:1024], rsd[:]]]
            U = {}
            for b in range(NB + 1):
                if b < NB:
                    hn = B[:, b * L:(b + 1) * L]
                    for j, (o, n) in enumerate(CH):
                        kg = pe.run(mm(ps[0:n, 3 + j, :], w1[:, l, HID + o:HID + o + n], hn), U.get(("g", j)))
                        ka = pe.run(mm(ps[0:n, j, :], w1[:, l, o:o + n], hn), U.get(("a", j)))
                        U["g", j] = sc.run(act(gl[j][0:n, :], ps[0:n, 3 + j, :], ACT.Gelu,
                                               bias=lcol(l, 6 + j)[0:n, :]), kg, U.get(("a", j)))
                        U["a", j] = ve.run(stt(hx[b % 2][j][0:n, :], ps[0:n, j, :], lcol(l, 3 + j)[0:n, :],
                                               gl[j][0:n, :], ALU.add, ALU.mult), ka, U["g", j], U.get(("y", b - 2)))
                        U["h", b] = U["a", j]
                if b >= 1:
                    c = b - 1
                    pe.wait(U["h", c], U.get(("x", c - 2)))
                    for j, (o, n) in enumerate(CH):
                        k = pe.run(mm(ps[:, 6 + c % 2, :], w2[0:n, l, j, :], hx[c % 2][j][0:n, :], j == 0, j == 2))
                    U["y", c] = k
                    x = X[:, c * L:(c + 1) * L]
                    U["x", c] = ve.run(stt(x, ps[:, 6 + c % 2, :], lcol(l, 2), x, ALU.add, ALU.add), k)
            barrier()

        st_out = [Dma(sem(f"s_o{i}")) for i in range(4)]
        last, fr, ot = {}, {}, {}
        for b in range(4):
            xtok[b] = load_x(b)
        gs = [P[:].rearrange("p g q -> p (g q)")[:, 0:512], P[:].rearrange("p g q -> p (g q)")[:, 512:1024],
              PT[:].rearrange("p g q -> p (g q)")[:, 0:512], PT[:].rearrange("p g q -> p (g q)")[:, 512:1024]]
        for b in range(NB):
            x, s, g, bk = X[:, b * L:(b + 1) * L], A[:, b * L:(b + 1) * L], gs[b % 4], b % 4
            pe.wait(fr.get(b - 4))
            for t in range(TPB):
                k = pe.run(tr(ps[:, bk, t * 128:(t + 1) * 128], x[:, t * 128:(t + 1) * 128], idf[:]))
            fr[b] = k = sc.run(act(g, ps[:, bk, :], ACT.Silu), k, ot.get(b - 4))
            k = ve.run(tt(g, g, s, ALU.mult), k)
            k = ve.run(tt(g, g, xt[b % 4], ALU.add), k, xtok[b])
            ot[b] = st_out[bk].start(sp, od[b], g.rearrange("p (t d) -> p t d", t=TPB), k)
            last[bk] = ot[b]
            if b + 4 < NB:
                xtok[b + 4] = load_x(b + 4, k)
        sp.wait(*last.values())

        block = ctx.enter_context(nc.Block())

        @block.tensor
        def _(e):
            pe.emit(e)

        @block.scalar
        def _(e):
            sc.emit(e)

        @block.vector
        def _(e):
            ve.emit(e)

        @block.gpsimd
        def _(e):
            po.emit(e)

        @block.sync
        def _(e):
            sp.emit(e)


def constants():
    f = np.float32
    half = np.arange(0, DH, 2, dtype=f)
    inv = (f(1.0) / np.power(f(10000.0), half / f(DH), dtype=f)).astype(f)
    t = np.arange(L, dtype=f)
    fr = (t[:, None] * inv[None, :]).astype(f)
    fr = np.concatenate([fr, fr], -1).astype(np.float64)
    base = (half + f(0.4 * DH)) / f(1.4 * DH)
    power = (t - f(L // 2)) / f(WIN // 2)
    scale = np.power(base[None, :].astype(np.float64), power[:, None].astype(np.float64))
    scale = np.concatenate([scale, scale], -1)
    cos, sin = np.cos(fr), np.sin(fr)
    sgn = np.concatenate([-np.ones(32), np.ones(32)])[None, :]
    tab = np.stack([np.stack([8 * cos * scale, 8 * sin * scale * sgn], 1),
                    np.stack([cos / scale, sin / scale * sgn], 1)], 0)
    tab = tab.reshape(2, TPB, 128, 2, DH).transpose(2, 0, 1, 3, 4).astype(f)
    q = np.arange(64)[:, None]
    k = np.arange(128)[None, :]
    ok = (k >= q) & (k <= q + 64)
    first = ok & (k >= 64)
    mask = np.zeros((2, 2, 64, 2, 2, 128), f)
    for v in range(2):
        for w in range(2):
            good = first if (v == 0 and w == 0) else ok
            mask[v, :, :, :, w, :] = np.where(good, 0.0, -1e30)[None, :, None, :]
    mask = mask.reshape(2, 128, 512).transpose(1, 0, 2)
    eye = np.eye(128, dtype=f)
    return tab, mask, eye


def kernel(**inputs):
    import ml_dtypes
    import concourse.bacc as bacc
    from concourse.bass_utils import run_bass_kernel_spmd as run

    a = {n.split("_", 2)[2]: np.ascontiguousarray(v) for n, v in inputs.items()}
    tab, mask, eye = constants()
    cols = np.zeros((128, 32), np.float32)
    cols[:, 0], cols[:, 1], cols[:, 2], cols[:, 3] = a["conv_b"], a["b_r"], a["b_i"], a["log_a"]
    cols[:, 4:8] = a["conv_w"][:, 0, :]
    w2 = np.zeros((128, DEPTH, 3, 128), np.float32)
    for l in range(DEPTH):
        c = cols[:, 8 + 9 * l:17 + 9 * l]
        c[:, 0], c[:, 1], c[:, 2] = a["ln_g"][l], a["ln_b"][l], a["b2"][l]
        for j, (o, n) in enumerate(CH):
            c[:n, 3 + j] = a["b1"][l, o:o + n]
            c[:n, 6 + j] = a["b1"][l, HID + o:HID + o + n]
            w2[:n, l, j, :] = a["w2"][l, o:o + n, :]
    feed = {
        "x": a["x"], "cols": cols, "idf": eye, "idb": eye.astype(ml_dtypes.bfloat16),
        "mask": mask.astype(ml_dtypes.bfloat16), "avg": np.full((128, 128), 1.0 / D, np.float32), "tab": tab,
        "wr": np.stack([a["W_r"].T, a["W_i"].T, a["W_out"].T], 1),
        "wqkv": a["wqkv"].transpose(1, 0, 2), "w1": a["w1"].transpose(1, 0, 2), "w2": w2,
        "wo": a["wo"].reshape(DEPTH, 4, 128, 128).transpose(2, 0, 1, 3),
        "gamma": a["gamma"], "q_scale": a["q_scale"], "k_scale": a["k_scale"],
    }
    feed = {n: np.ascontiguousarray(v) for n, v in feed.items()}
    nc = bacc.Bacc("TRN2", target_bir_lowering=False, num_devices=1)
    d = {n: nc.dram_tensor(f"in_{n}", v.shape, mybir.dt.from_np(v.dtype), kind="ExternalInput").ap() for n, v in feed.items()}
    out = nc.dram_tensor("out_0", (NB, L, D), F32, kind="ExternalOutput").ap()
    program(nc, d, out)
    r = run(nc, [{f"in_{n}": v for n, v in feed.items()}], core_ids=[0])
    return r.results[0]["out_0"]
```

```python
from contextlib import ExitStack

import numpy as np

import concourse.bass as bass
from concourse import mybir

F32 = mybir.dt.float32
BF16 = mybir.dt.bfloat16
F32R = mybir.dt.float32r
ALU = mybir.AluOpType
ACT = mybir.ActivationFunctionType
AX = mybir.AxisListType.X

NB, L, D = 16, 512, 128
TPB = L // 128
NT = NB * TPB
DEPTH, HEADS, DH, WIN = 2, 8, 64, 64
INNER = HEADS * DH
HID = 341
CH = [(0, 128), (128, 128), (256, 85)]
LN_EPS = 1e-5
RMS_EPS = 1e-6
LN2 = 0.6931471805599453


class Queue:

    def __init__(self, sem):
        self.sem, self.items, self.count, self.seen, self.last = sem, [], 0, {}, None

    def wait(self, *toks):
        for t in toks:
            if t is not None and self.seen.get(id(t[0]), 0) < t[1]:
                self.seen[id(t[0])] = t[1]
                self.items.append(lambda e, t=t: e.wait_ge(t[0], t[1]))

    def put(self, ins):
        self.items.append(ins)

    def run(self, ins, *waits):
        self.wait(*waits)
        self.count += 1
        self.last = (self.sem, self.count)
        self.items.append(lambda e: ins(e).then_inc(self.sem, 1))
        return self.last

    def emit(self, e):
        for i in self.items:
            i(e)


class Dma:

    def __init__(self, sem):
        self.sem, self.count = sem, 0

    def start(self, q, out, in_, *waits):
        q.wait(*waits)
        self.count += 16
        q.put(lambda e: e.dma_start(out, in_).then_inc(self.sem, 16))
        return (self.sem, self.count)


def mm(out, lhsT, rhs, start=True, stop=True):
    return lambda e: e.matmul(out, lhsT, rhs, start=start, stop=stop, skip_group_check=True)


def tr(out, in_, ident):
    return lambda e: e.transpose(out, in_, ident)


def act(out, in_, f, **kw):
    return lambda e: e.activation(out, in_, f, **kw)


def tt(out, a, b, op):
    return lambda e: e.tensor_tensor(out, a, b, op)


def ts(out, a, s1, s2, op0, op1=None):
    if op1 is None:
        return lambda e: e.tensor_scalar(out, a, s1, None, op0)
    return lambda e: e.tensor_scalar(out, a, s1, s2, op0, op1)


def stt(out, a, s, b, op0, op1):
    return lambda e: e.scalar_tensor_tensor(out, a, s, b, op0, op1)


def cp(out, a):
    return lambda e: e.tensor_copy(out, a)


def zero(out, v=0.0):
    return lambda e: e.memset(out, v)


def program(nc, d, out):
    ctx = ExitStack()
    with ctx:
        def sb(name, shape, dt=F32):
            return ctx.enter_context(nc.sbuf_tensor(name, shape, dt))

        def sem(name):
            return ctx.enter_context(nc.semaphore(name))

        pe, sc, ve, po, sp = (Queue(sem(n)) for n in ("s_pe", "s_act", "s_dve", "s_pool", "s_sp"))

        X = sb("X", [128, NB * L])
        A = sb("A", [128, NB * L])
        B = sb("B", [128, NB * L])
        wqkv = sb("wqkv", [128, 2, 3 * INNER], F32R)
        wo = sb("wo", [128, DEPTH, 4, 128])
        w1 = sb("w1", [128, 2 * HID])
        w2 = sb("w2", [128, 3, 128])
        wr = sb("wr", [128, 3, 128])
        tabl = sb("tabl", [128, 2, TPB, 2, DH])
        cols = sb("cols", [128, 32])
        gam = sb("gam", [128, 128])
        idf = sb("idf", [128, 128])
        idb = sb("idb", [128, 128], BF16)
        avg = sb("avg", [128, 128])
        mask = sb("mask", [128, 2, 512], BF16)
        cst = sb("cst", [128, 8])
        ab = sb("ab", [128, 16])
        st = sb("st", [128, 4, 6])
        mv = sb("mv", [128, TPB, 2])
        rst = sb("rst", [128, TPB])
        ro = sb("ro", [128, TPB])
        ss = sb("ss", [128, 16])
        rr = sb("rr", [128, 16])
        nm = sb("nm", [128, 8])
        den = sb("den", [128, 8])
        rden = sb("rden", [128, 8])
        oT = sb("oT", [128, 4, L])
        h2, sq, rsd = (sb(n_, [128, L]) for n_ in ("h2", "sq", "rsd"))
        sqr = sb("sqr", [128, 2, L], F32R)
        avgr = sb("avgr", [128, 128], F32R)
        side = sb("side", [128, 3, L])
        ps = ctx.enter_context(nc.psum_tensor("ps", [128, 8, 512], F32))

        CB, BR, BI, LA, CW = (cols[:, i:i + 1] for i in range(5))
        cw = [cols[:, 4 + j:5 + j] for j in range(4)]

        def lcol(l, j):
            return cols[:, 8 + 9 * l + j:9 + 9 * l + j]

        one, eps_ln, eps_rms, ln2x8, mln2 = (cst[:, i:i + 1] for i in range(5))

        ld = Dma(sem("s_ld"))
        lw = Dma(sem("s_lw"))
        lt = Dma(sem("s_tab"))
        lq = Dma(sem("s_qks"))
        ring = [Dma(sem(f"s_x{i}")) for i in range(2)]
        xd = d["x"].rearrange("b (t p) d -> b p t d", p=128)
        od = out.rearrange("b (t p) d -> b p t d", p=128)

        def load_x(b, buf, *waits):
            return ring[b % 2].start(sp, buf.rearrange("p (t d) -> p t d", t=TPB), xd[b], *waits)

        xr = [side[:, 0, :], side[:, 1, :]]
        xnb = side[:, 2, :]
        def load_tables(l, buf):
            qv = buf.rearrange("p (i s e) -> p i s e", i=2, s=2)
            tb = lt.start(sp, tabl[:], d["tab"])
            for i, n in enumerate(("q_scale", "k_scale")):
                lq.start(sp, qv[:, i, 0, :], d[n][l].partition_broadcast(128))
                lq.start(sp, qv[:, i, 1, 0:32], d[n][l, 32:64].partition_broadcast(128))
                qt = lq.start(sp, qv[:, i, 1, 32:64], d[n][l, 0:32].partition_broadcast(128))
            return qv, tb, qt

        xtok = {0: load_x(0, xr[0])}
        small = ld.start(sp, idf[:], d["idf"])
        wraw = B[:, 0:3 * INNER]
        wq0 = [Dma(sem(f"s_w{c}")).start(sp, wraw[:, c * 512:(c + 1) * 512], d["wqkv"][:, 0, c * 512:(c + 1) * 512])
               for c in range(3)]
        tab0 = load_tables(0, B[:, 2048:2304])
        xtok[1] = load_x(1, xr[1])
        lm = Dma(sem("s_mask"))
        for t_, n in ((idb, "idb"), (mask, "mask"), (cols, "cols")):
            masks = lm.start(sp, t_[:], d[n])
        for t_, n in ((avg, "avg"), (wo, "wo"), (wr, "wr")):
            big = lw.start(sp, t_[:], d[n])

        def load_w12(l, *waits):
            lw.start(sp, w1[:], d["w1"][:, l, :], *waits)
            return lw.start(sp, w2[:], d["w2"][:, l])

        W = {("w12", 0): load_w12(0)}
        big = lw.start(sp, gam[:], d["gamma"].partition_broadcast(128))

        for i, v in enumerate((1.0, LN_EPS, RMS_EPS, 8 * LN2, -LN2)):
            ve.run(zero(cst[:, i:i + 1], v))
        consts = ve.run(zero(h2[64:128, 0:1]))

        def split(hi, lo, x, ehi, elo, *waits, whi=()):
            k = ehi.run(act(hi, x, ACT.Copy) if ehi is sc else cp(hi, x), *waits, *whi)
            return k, elo.run(tt(lo, x, hi.bitcast(F32), ALU.subtract), k, *waits)

        def lasts():
            return [q.last for q in (pe, sc, ve, po) if q.last]

        def barrier(toks):
            for q in (sc, ve, po, sp):
                q.wait(*toks)

        ATTN = "natural_log_exp_and_others"
        sc.put(lambda e: e.preload_act_table_set(ATTN))
        sc.wait(consts)

        F, U = {}, {}

        ax, ez, u, dd, lnu, ru, half, nx, mx = (ab[:, i:i + 1] for i in range(9))
        hbr, hbi = ab[:, 9:10], ab[:, 10:11]
        def set_decay(part):
            if part == 0:
                ve.run(ts(nx, LA, -1.0, None, ALU.mult), masks)
                ve.run(ts(mx, nx, 0.0, None, ALU.max), ve.last)
                k = ve.run(tt(ax, LA, nx, ALU.max))
                F["ez"] = sc.run(act(ez, ax, ACT.Exp, scale=-1.0), k)
            if part == 1:
                k = ve.run(ts(u, ez, 1.0, None, ALU.add), F["ez"])
                F["lnu"] = sc.run(act(lnu, u, ACT.Ln), k)
                ve.run(lambda e: e.reciprocal(ru, u), k)
                k = ve.run(ts(dd, u, -1.0, None, ALU.add))
                ve.run(tt(dd, ez, dd, ALU.subtract), k)
            if part == 2:
                k = ve.run(stt(dd, dd, ru, lnu, ALU.mult, ALU.add), ve.last, F["lnu"])
                k = ve.run(tt(dd, dd, mx, ALU.add), k)
                F["decay"] = ve.run(ts(half, dd, -4.0, None, ALU.mult), k)
                ve.run(ts(hbr, BR, 0.5, None, ALU.mult))
                ve.run(ts(hbi, BI, 0.5, None, ALU.mult))

        def ln_stats(b):
            xb = xr[b % 2].rearrange("p (t d) -> p t d", t=TPB)
            ve.wait(xtok[b])
            for t in range(TPB):
                k = ve.run(lambda e, t=t: e.bn_stats(st[:, t, :], xb[:, t, :]))
            ve.wait(k, F.get(("ln", b - 1)), F.get(("nrm", b - 1)))
            for t in range(TPB):
                k = ve.run(lambda e, t=t: e.bn_aggr(mv[:, t, :], st[:, t, :]))
            F["st", b] = k

        def ln_root(b):
            k = sc.run(act(rst[:], mv[:, :, 1], ACT.Ln, bias=eps_ln), F["st", b], F.get(("nrm", b - 1)))
            F["ln", b] = sc.run(act(rst[:], rst[:], ACT.Exp, scale=-0.5), k)

        def ln_apply(b):
            xb = xr[b % 2].rearrange("p (t d) -> p t d", t=TPB)
            ve.wait(F["ln", b], F.get(("tx", b - 1)))
            for t in range(TPB):
                k = ve.run(ts(xnb[:, t * 128:(t + 1) * 128], xb[:, t, :], mv[:, t, 0:1], rst[:, t:t + 1],
                              ALU.subtract, ALU.mult))
            F["nrm", b] = k
            if b + 2 < NB:
                xtok[b + 2] = load_x(b + 2, xr[b % 2], k)

        def ln_turn(b, bank, *waits):
            pe.wait(F["nrm", b], small, *waits)
            for t in range(TPB):
                k = pe.run(tr(ps[:, bank, t * 128:(t + 1) * 128], xnb[:, t * 128:(t + 1) * 128], idf[:]))
            F["tx", b] = k
            F["lnbank", b] = bank

        def ln_keep(b):
            F["x", b] = sc.run(act(X[:, b * L:(b + 1) * L], ps[:, F["lnbank", b], :], ACT.Copy), F["tx", b])
            return F["x", b]

        def ln_copy(b):
            F["xa", b] = sc.run(act(A[:, b * L:(b + 1) * L], X[:, b * L:(b + 1) * L], ACT.Copy), F["x", b])

        def conv(b, y):
            x = A[:, b * L:(b + 1) * L]
            k = ve.run(ts(y, x, cw[3], CB, ALU.mult, ALU.add), F["xa", b], U.get(("xi", b - 2)))
            for j in (2, 1, 0):
                k = ve.run(stt(y[:, 3 - j:], x[:, :L - 3 + j], cw[j], y[:, 3 - j:], ALU.mult, ALU.add), k)
            F["cv", b] = k

        wk = [side[:, 0, :], side[:, 1, :]]

        def rec_decay(b):
            r, w = B[:, b * L:(b + 1) * L], wk[b % 2]
            F["a", b] = sc.run(act(r, r, ACT.Exp, scale=half, bias=half), F["decay"])

        def rec_a2(b):
            r, w = B[:, b * L:(b + 1) * L], wk[b % 2]
            F["a2", b] = po.run(tt(w, r, r, ALU.mult), F["a", b], F.get(("in", b - 2)), F.get(("sum", b - 2)))

        def rec_root(b):
            w = wk[b % 2]
            F["a2n", b] = ve.run(ts(w, w, 1.0, -1.0, ALU.min, ALU.mult), F["a2", b])

        def rec_root2(b):
            w = wk[b % 2]
            k = sc.run(act(w, w, ACT.Ln, bias=one), F["a2n", b])
            F["rt", b] = sc.run(act(w, w, ACT.Exp, scale=0.5, bias=mln2), k)

        def rec_input(b):
            a = A[:, b * L:(b + 1) * L]
            F["in", b] = po.run(tt(a, a, wk[b % 2], ALU.mult), F["rt", b])

        def rec_scan(b):
            a, r = A[:, b * L:(b + 1) * L], B[:, b * L:(b + 1) * L]
            F["hs", b] = ve.run(lambda e: e.tensor_tensor_scan(a, r, a, 0.0, ALU.mult, ALU.add), F["in", b])

        def rec_out(b, bank, *waits):
            a = A[:, b * L:(b + 1) * L]
            pe.wait(F["hs", b], *waits)
            for t in range(TPB):
                k = pe.run(mm(ps[:, bank, t * 128:(t + 1) * 128], a[:, t * 128:(t + 1) * 128], wr[:, 2, :]))
            F["mmo", b], F["obank", b] = k, bank

        def rec_keep(b):
            F["out", b] = sc.run(act(A[:, b * L:(b + 1) * L], ps[:, F["obank", b], :], ACT.Copy), F["mmo", b])
            return F["out", b]

        def rec_square(b):
            F["sqo", b] = sc.run(act(xnb, A[:, b * L:(b + 1) * L], ACT.Square), F["out", b], F.get(("sum", b - 1)))

        def rec_sum(b):
            k = ve.run(lambda e: e.tensor_reduce(ro[:], xnb.rearrange("p (t d) -> p t d", t=TPB), AX, ALU.add),
                       F["sqo", b], F.get(("s", b - 1)))
            F["sum", b] = k

        def rec_rms(b):
            k = sc.run(act(ro[:], ro[:], ACT.Ln, scale=1.0 / D, bias=eps_rms), F["sum", b])
            F["rms", b] = sc.run(act(ro[:], ro[:], ACT.Exp, scale=-0.5), k)

        def rec_scale(b):
            ve.wait(F["rms", b], F["ghalf"])
            for t in range(TPB):
                a = A[:, b * L + t * 128:b * L + (t + 1) * 128]
                F["s", b] = ve.run(stt(a, a, ro[:, t:t + 1], gam[:], ALU.mult, ALU.mult))


        def split_wqkv(c, x, *waits):
            n = slice(c * 512, (c + 1) * 512)
            W["wqkv", c] = split(wqkv[:, 0, n], wqkv[:, 1, n], x, sc, ve, *waits)[1]

        def set_tables(qv, tb, qt):
            for i in range(2):
                for s in range(2):
                    k = ve.run(tt(tabl[:, i, :, s, :], tabl[:, i, :, s, :],
                                  qv[:, i, s, :].unsqueeze(1).to_broadcast([128, TPB, DH]), ALU.mult), qt, tb)
            return k

        ln_stats(0)
        ln_root(0)
        ln_apply(0)
        for c in range(2):
            split_wqkv(c, wraw[:, c * 512:(c + 1) * 512], wq0[c])
        ln_turn(0, 7)
        ln_keep(0)
        vs_lo = [Dma(sem(f"s_vl{t}")) for t in range(TPB)]
        vs_hi = [Dma(sem(f"s_vh{t}")) for t in range(TPB)]
        hT = sb("hT", [128, 2, 2, L], F32R)
        hzero = ve.run(zero(hT[64:128, :, :, 0:1].bitcast(F32)))

        def sp_(name, shape, dt=F32):
            return phase.enter_context(nc.sbuf_tensor(name, shape, dt))

        with ExitStack() as phase:
            t1, t2, t3, sqk = (sp_(n_, [128, 1024]) for n_ in ("t1", "t2", "t3", "sqk"))
            P, PT, qbd = (sp_(n_, [128, 8, 128]) for n_ in ("P", "PT", "qbd"))
            kT = sp_("kT", [128, 4, 64 + 256])
            Vn, Vs = (sp_(n_, [128, TPB, INNER]) for n_ in ("Vn", "Vs"))
        tq = [t1, t3]
        with ExitStack() as phase:
            w1r = sp_("w1r", [128, 2, 2 * HID], F32R)
            hnr = sp_("hnr", [128, 2, 2, L], F32R)
            room = sp_("room", [128, 4096 - 4 * HID - 4 * L])
            hxf = sp_("hxf", [128, 3, L])
            hx = sp_("hx", [128, 2, 3, 2, L], F32R)
            w2r = sp_("w2r", [128, 2, 3, 128], F32R)
        xg, qs = oT, oT[:, 2, 0:256]
        gl = [side[:, 0, :], side[:, 1, :], room[:, 0:L]]
        ti = [xg[:, i, :] for i in range(2)]
        cv = [xg[:, 3, :], side[:, 2, :]]
        THREE = ((1, 0), (0, 1), (0, 0))
        T = {}
        for l in range(DEPTH):
            if l:
                sc.put(lambda e: e.preload_act_table_set(ATTN))
                ffn = lasts()
                add_qk(0)
                norm_rt(0)
                scale_qk(0)
                barrier(ffn)
                pe.wait(U["side"])
                banks = [U["x", NB - 1], *(U[n_, j] for n_ in "ag" for j in range(3))]
            U.clear()

            def vbank(i):
                return 2 if i % 2 else 7

            def obank(i):
                return vbank(i + 4)

            def bank(i):
                return vbank(i) if i < NT + 3 else 7

            def spare(i):
                if i >= NT + 3:
                    return (U.get("side"),)
                return T.get(("v", min(i, NT - 1))), T.get(("o", min(i - 4, NT - 1))), T.get(("misc", i - 2))

            HALF = (slice(0, 64), 0), (slice(64, 128), 1)

            def shift_in(b):
                x = X[:, b * L:(b + 1) * L]
                ve.wait(T.get(("vm", 4 * b - 5)), F["x", b])
                for p, o in HALF:
                    T["hi", b] = ve.run(cp(hT[p, b % 2, 0, o:], x[p, 0:L - o]))

            def shift_rest(b):
                x = X[:, b * L:(b + 1) * L]
                for p, o in HALF:
                    T["h", b] = ve.run(tt(hT[p, b % 2, 1, o:], x[p, 0:L - o], hT[p, b % 2, 0, o:].bitcast(F32), ALU.subtract),
                                       T["hi", b])

            def turn_qk(i):
                c0 = tq[i % 2][:]
                pe.wait(T["tn", i], T.get(("PT", i - 2)))
                for bank in (5, 6):
                    for c in range(4):
                        m = 4 * (bank - 5) + c
                        k = pe.run(tr(ps[:, bank, c * 128:(c + 1) * 128], c0[:, m * 128:(m + 1) * 128], idf[:]))
                    T["tp", i, bank] = k
                T["tqk", i] = k

            def keep_q(i):
                src = ps[:, 5, :].rearrange("p (g q) -> p g q", q=64)
                sc.run(act(qbd[0:64, :, 0:64], src[0:64], ACT.Copy), T["tp", i, 5], zeros, T.get(("sim", i - 1)))
                T["qk", i] = sc.run(act(qbd[64:128, :, 64:128], src[64:128], ACT.Copy))

            def keep_k(i):
                t = i % TPB
                s0 = 64 + (t % 2) * 128
                ve.wait(T["tp", i, 6], T.get(("sim", i - 1)))
                if t == 2:
                    ve.run(cp(kT[:, :, 0:64], kT[:, :, 256:320]), T["kt", i - 1])
                T["kt", i] = ve.run(cp(kT[:, :, s0:s0 + 128], ps[:, 6, :].rearrange("p (c q) -> p c q", c=4)))

            def product(o, b, t, n):
                pe.wait(W["wqkv", n])
                for j, (p, q) in enumerate(((1, 0), (0, 1), (0, 0))):
                    k = pe.run(mm(o, hT[:, b % 2, p, t * 128:(t + 1) * 128], wqkv[:, q, n * 512:(n + 1) * 512], j == 0, j == 2))
                return k

            def qk_proj(i):
                b, t = divmod(i, TPB)
                pe.wait(T["h", b], T.get(("t2", i - 1)), hzero)
                for n in range(2):
                    k = product(ps[:, n, :], b, t, n)
                T["qkv", i] = k

            def square(i):
                s2 = sqk[:].rearrange("p (h e) -> p h e", e=DH)
                s16 = ps[:, 0:2, :].rearrange("p i (h e) -> p (i h) e", e=DH)
                T["s2", i] = sc.run(act(s2, s16, ACT.Square), T["qkv", i], T.get(("ss", i - 1)))

            def norm_sum(i):
                s2 = sqk[:].rearrange("p (h e) -> p h e", e=DH)
                k = ve.run(lambda e: e.tensor_reduce(ss[:], s2, AX, ALU.add), T["s2", i], T.get(("rr", i - 1)))
                T["ss", i] = ve.run(ts(ss[:], ss[:], 1e-24, None, ALU.max), k)

            def rotate(i, part):
                t = i % TPB
                r1 = tq[i % 2]
                qk = ps[:, 0:2, :].rearrange("p i (h e) -> p i h e", e=DH)
                o1 = r1[:].rearrange("p (i h e) -> p i h e", i=2, e=DH)
                o2 = t2[:].rearrange("p (i h e) -> p i h e", i=2, e=DH)
                if part == 0:
                    C = tabl[:, :, t, 0, :].unsqueeze(2).to_broadcast([128, 2, HEADS, DH])
                    ve.run(tt(o1, qk, C, ALU.mult), T["s2", i], T.get(("tqk", i - 2)), tabk if i == 0 else None)
                    return
                S, s = tabl[:, :, t, 1, :], part - 1
                T["t2", i] = ve.run(tt(o2[:, :, :, 32 * s:32 * s + 32], qk[:, :, :, 32 - 32 * s:64 - 32 * s],
                                       S[:, :, 32 * s:32 * s + 32].unsqueeze(2).to_broadcast([128, 2, HEADS, 32]), ALU.mult),
                                    T.get(("add", i - 1)))

            def add_qk(i):
                r1 = tq[i % 2]
                T["add", i] = po.run(tt(r1[:], r1[:], t2[:], ALU.add), T["t2", i])

            def v_proj(i):
                b, t = divmod(i, TPB)
                pe.wait(T["h", b], F["x", b], T.get(("misc", i - 2)), T.get(("v", i - 1)), T.get(("o", i - 4)))
                T["vm", i] = product(ps[:, vbank(i), :], b, t, 2)

            def keep_v(i):
                t = i % TPB
                T["v", i] = sc.run(act(Vn[:, t, :], ps[:, vbank(i), :], ACT.Copy), T["vm", i], T.get(("av", i - 4)),
                                   T.get(("vs", i - 4)), T.get(("vslo", i - 3)))
                shift_v(i)

            def shift_v(i):
                t = i % TPB
                if t > 0:
                    T["vslo", i] = vs_lo[t].start(sp, Vs[0:64, t, :], Vn[64:128, t - 1, :], T["v", i], T.get(("av", i - 4)))
                T["vs", i] = vs_hi[t].start(sp, Vs[64:128, t, :], Vn[0:64, t, :], T["v", i], T.get(("av", i - 4)))

            def norm_rt(i):
                k = sc.run(act(rr[:], ss[:], ACT.Ln, scale=65536.0), T["ss", i], T.get(("tn", i - 1)))
                T["rr", i] = sc.run(act(rr[:], rr[:], ACT.Exp, scale=-0.5, bias=ln2x8), k)

            def scale_qk(i):
                v = tq[i % 2][:].rearrange("p (h e) -> p h e", e=DH)
                T["tn", i] = po.run(tt(v, v, rr[:].unsqueeze(2).to_broadcast([128, 16, DH]), ALU.mult),
                                    T["add", i], T["rr", i])

            def turn_p(i):
                pe.wait(T.get(("qk", i + 1)), T.get(("kt", i + 1)))
                for g in range(8):
                    pe.wait(T["pn", i, g // 4])
                    k = pe.run(tr(ps[:, 5 + g // 4, (g % 4) * 128:(g % 4 + 1) * 128], P[:, g, :], idf[:]))
                T["tp2", i] = k

            def keep_p(i):
                T["PT", i] = sc.run(act(PT[:], ps[:, 5:7, :].rearrange("p s (g q) -> p (s g) q", g=4), ACT.Copy),
                                    T["tp2", i], T.get(("av", i - 1)))

            def sims(i):
                t = i % TPB
                pe.wait(T["qk", i], T["kt", i], masks)
                for s in range(2):
                    pe.wait(T.get(("e", i - 1, s)))
                    pe.put(mm(ps[:, 3 + s, :], idb[:], mask[:, min(t, 1), :], True, False))
                    for c in (2 * s, 2 * s + 1):
                        for w in range(2):
                            g = 2 * c + w
                            k0 = (t % 2) * 128 + w * 64
                            k = pe.run(mm(ps[:, 3 + s, (g % 4) * 128:(g % 4 + 1) * 128], qbd[:, g, :],
                                          kT[:, c, k0:k0 + 128], False, True))
                    T["sim", i, s] = k
                T["sim", i] = k

            def row_max(i, s):
                S4 = ps[:, 3 + s, :].rearrange("p (g k) -> p g k", g=4)
                T["nm", i, s] = ve.run(lambda e: e.tensor_reduce(nm[:, 4 * s:4 * s + 4], S4, AX, ALU.max, negate=True),
                                       T["sim", i, s], T.get(("e", i - 1, s)))

            def exps(i, s):
                sc.wait(T.get(("tp2", i - 1)), T.get(("rd", i - 1, s)), T["nm", i, s])
                for g in range(4 * s, 4 * s + 4):
                    k = sc.run(act(P[:, g, :], ps[:, 3 + s, (g % 4) * 128:(g % 4 + 1) * 128], ACT.Exp,
                                   bias=nm[:, g:g + 1], accum_out=den[:, g:g + 1]))
                T["e", i, s] = k

            def invert(i, s):
                T["rd", i, s] = ve.run(lambda e: e.reciprocal(rden[:, 4 * s:4 * s + 4], den[:, 4 * s:4 * s + 4]),
                                       T["e", i, s], T.get(("pn", i - 1, s)))

            def normalise(i, s):
                g = slice(4 * s, 4 * s + 4)
                T["pn", i, s] = po.run(tt(P[:, g, :], P[:, g, :], rden[:, g].unsqueeze(2).to_broadcast([128, 4, 128]),
                                          ALU.mult), T["rd", i, s])

            def attend(i):
                b, t = divmod(i, TPB)
                pe.wait(T["PT", i], T["v", i], T["vs", i], T.get(("vslo", i)), T.get(("o", i - 1)), T.get(("v", i + 2)), T.get(("misc", i + 2)), vzero)
                for c in range(4):
                    for w in range(2):
                        for hh in range(2):
                            V = Vn if w else Vs
                            h = 2 * c + hh
                            k = pe.run(mm(ps[64 * hh:64 * hh + 64, obank(i), c * 128 + w * 64:c * 128 + w * 64 + 64],
                                          V[:, t, h * DH:(h + 1) * DH], PT[:, 2 * c + w, 64 * hh:64 * hh + 64]))
                T["av", i] = k

            def keep_o(i):
                b, t = divmod(i, TPB)
                T["o", i] = sc.run(act(oT[:, :, t * 128:(t + 1) * 128],
                                       ps[:, obank(i), :].rearrange("p (c q) -> p c q", c=4), ACT.Copy),
                                   T["av", i], T.get(("wo", b - 1, t // 2)))

            def proj(b, z, u):
                c0 = u * 256
                pe.wait(T["o", 4 * b + 1 + 2 * u], big, *spare(z))
                for c in range(4):
                    k = pe.run(mm(ps[:, bank(z), 0:256], wo[:, l, c, :], oT[:, c, c0:c0 + 256], c == 0, c == 3))
                T["wo", b, u] = k

            def proj_add(b, z, u):
                x = X[:, b * L + u * 256:b * L + u * 256 + 256]
                T["misc", z] = U["side"] = T["xa", b] = ve.run(tt(x, ps[:, bank(z), 0:256], x, ALU.add), T["wo", b, u], F["xa", b] if l == 0 else None)

            def shift_h2(b):
                x = X[:, b * L:(b + 1) * L]
                ve.run(cp(h2[0:64, :], x[0:64, :]), T["xa", b], T.get(("hc", b - 1)))
                T["h2", b] = ve.run(cp(h2[64:128, 1:L], x[64:128, 0:L - 1]))

            def mean(b, z):
                T["mu", b] = pe.run(mm(ps[:, bank(z), :], avg[:], h2[:]), T["h2", b], *spare(z))

            def centre(b, z):
                T["misc", z] = U["side"] = T["hc", b] = ve.run(tt(sq[:], h2[:], ps[:, bank(z), :], ALU.subtract), T["mu", b])

            def square_hc(b):
                T["sqh", b] = sc.run(act(sqr[:, 0, :], sq[:], ACT.Square), T["hc", b], T.get(("va", b - 1)))
                T["sqf", b] = po.run(tt(rsd[:], sq[:], sq[:], ALU.mult), T["hc", b], T.get(("hn", b - 1)))

            def square_lo(b):
                T["sq", b] = ve.run(tt(sqr[:, 1, :], rsd[:], sqr[:, 0, :].bitcast(F32), ALU.subtract),
                                    T["sqh", b], T["sqf", b], T.get(("va", b - 1)))

            def var(b, z):
                pe.wait(T["sq", b], avg_r, *spare(z))
                for p in (1, 0):
                    k = pe.run(mm(ps[:, bank(z), :], avgr[:], sqr[:, p, :], p == 1, p == 0))
                T["va", b] = k

            def root_var(b, z):
                k = sc.run(act(rsd[:], ps[:, bank(z), :], ACT.Ln, bias=eps_ln), T["va", b])
                T["misc", z] = U["side"] = k
                T["rs", b] = sc.run(act(rsd[:], rsd[:], ACT.Exp, scale=-0.5), k)

            def scale_hc(b):
                hn = B[:, b * L:(b + 1) * L]
                k = ve.run(tt(hn, sq[:], rsd[:], ALU.mult), T["rs", b], F.get(("hs", b)))
                T["hn", b] = ve.run(ts(hn, hn, lcol(l, 0), lcol(l, 1), ALU.mult, ALU.add), k)

            def keep_misc(b, z):
                T["misc", z] = (ln_keep if l == 0 else rec_keep)(b)

            def split_hn(b):
                U["hi", b], U["lo", b] = split(hnr[:, b % 2, 0, :], hnr[:, b % 2, 1, :], B[:, b * L:(b + 1) * L], sc, po,
                                               T["hn", b], U.get(("hn", b - 2)))

            def split_hx(b, j):
                n = CH[j][1]
                U["xl", j] = split(hx[0:n, b % 2, j, 0, :], hx[0:n, b % 2, j, 1, :], hxf[0:n, j, :], sc, po,
                                       U["a", j], U.get(("y", b - 2)))[1]
                U["h", b] = U["xl", j]

            def up(b):
                pe.wait(U["w1"], U["lo", b])

                def three(bank, o, n):
                    for c, (p, q) in enumerate(THREE):
                        k = pe.run(mm(ps[0:n, bank, :], w1r[:, q, o:o + n], hnr[:, b % 2, p, :], c == 0, c == 2))
                    return k

                for j, (o, n) in enumerate(CH):
                    pe.wait(U.get(("g", j)))
                    kg = three(3 + j, HID + o, n)
                    pe.wait(U.get(("a", j)))
                    ka = three(j, o, n)
                    U["g", j] = sc.run(act(gl[j][0:n, :], ps[0:n, 3 + j, :], ACT.Gelu, bias=lcol(l, 6 + j)[0:n, :]),
                                       kg, U.get(("a", j)))
                    U["a", j] = ve.run(stt(hxf[0:n, j, :], ps[0:n, j, :], lcol(l, 3 + j)[0:n, :],
                                           gl[j][0:n, :], ALU.add, ALU.mult), ka, U["g", j], U.get(("xl", j)))
                U["hn", b] = ka
                for j in range(3):
                    split_hx(b, j)

            def down(b):
                pe.wait(U["h", b], U["w2"], U.get(("x", b - 1)))
                for j, (o, n) in enumerate(CH):
                    for c, (p, q) in enumerate(THREE):
                        k = pe.run(mm(ps[:, 6, :], w2r[0:n, q, j, :], hx[0:n, b % 2, j, p, :], j + c == 0, j + c == 4))
                U["y", b] = k
                x = X[:, b * L:(b + 1) * L]
                F["x", b] = U["x", b] = ve.run(stt(x, ps[:, 6, :], lcol(l, 2), x, ALU.add, ALU.add), k)

            def gates(b):
                xc, r = cv[b % 2], B[:, b * L:(b + 1) * L]
                k = pe.run(mm(ps[:, 7, :], wr[:, 0, :], xc), F["cv", b], U.get("side"), big)
                F["r", b] = k = sc.run(act(r, ps[:, 7, :], ACT.Tanh, scale=0.5, bias=hbr), k, U["lo", b])
                U["side"] = k

            def gates2(b):
                xc, xi = cv[b % 2], A[:, b * L:(b + 1) * L]
                k = pe.run(mm(ps[:, 7, :], wr[:, 1, :], xc), U["side"])
                U["side"] = k = sc.run(act(ti[b % 2], ps[:, 7, :], ACT.Tanh, scale=0.5, bias=hbi), k, U.get(("xi", b - 2)))
                U["xi", b] = ve.run(stt(xi, ti[b % 2], 1.0, xc, ALU.add, ALU.mult), k)

            xe = [xg[:, i, :] for i in range(2)]
            ge = [xg[:, 2 + i, :] for i in range(2)]

            def end_turn(b):
                x = X[:, b * L:(b + 1) * L]
                pe.wait(U["x", b], U.get("side"))
                for t in range(TPB):
                    k = pe.run(tr(ps[:, 7, t * 128:(t + 1) * 128], x[:, t * 128:(t + 1) * 128], idf[:]))
                U["th", b] = sc.run(act(ge[b % 2], ps[:, 7, :], ACT.Tanh, scale=0.5), k, U.get(("st", b - 2)))

            def end_out(b):
                g = ge[b % 2]
                k = ve.run(stt(g, g, 1.0, ps[:, 7, :], ALU.add, ALU.mult), U["th", b])
                U["side"] = k
                k = ve.run(tt(g, g, A[:, b * L:(b + 1) * L], ALU.mult), k, F["s", b])
                k = ve.run(tt(g, g, xe[b % 2], ALU.add), k, xtok[b])
                U["st", b] = st_out[b % 2].start(sp, od[b], g.rearrange("p (t d) -> p t d", t=TPB), k)
                if b + 2 < NB:
                    xtok[b + 2] = load_x(b + 2, xe[b % 2], k)

            if l == 0:
                shift_in(0)
                shift_rest(0)
                qk_proj(0)
                tabk = set_tables(*tab0)
                ln_stats(1)
                ln_root(1)
                square(0)
                ln_apply(1)
                for p in range(3):
                    rotate(0, p)
                split_wqkv(2, wraw[:, 1024:1536], wq0[2])
                norm_sum(0)
            po.run(zero(kT[:, :, 0:64]))
            vzero = po.run(zero(Vs[0:64, 0, :]))
            zeros = po.run(zero(qbd[:]))
            for i in range(NT + 3):
                m, j, n = i - 1, i - 2, i - 3

                def at(f, first, *args):
                    b, r = divmod(i - first, 4)
                    if r == 0 and 0 <= b < NB:
                        f(b, *args)

                def early(f, first, *args):
                    b, r = divmod(i - first, 4)
                    if r == 0 and 2 <= b < NB:
                        f(b, *args)

                if l and i == 1:
                    pe.wait(*banks)
                if 0 <= n < NT:
                    turn_p(n)
                if 0 < i < NT:
                    rotate(i, 0)
                at(centre, 9, i - 1)
                at(proj_add, 6, i - 1, 0)
                at(proj_add, 8, i - 1, 1)
                if l == 0:
                    early(ln_turn, -6, vbank(i), T.get(("o", i - 4)), T.get(("misc", i - 2)))
                    if i == 1:
                        ln_turn(1, vbank(i))
                else:
                    at(rec_out, 6, vbank(i), T.get(("o", i - 4)), T.get(("misc", i - 2)))
                if 0 <= n < NT:
                    keep_p(n)
                if l == 0:
                    early(keep_misc, -6, i - 2)
                    if i == 1:
                        keep_misc(1, i - 2)
                else:
                    at(keep_misc, 6, i - 2)
                at(root_var, 11, i - 1)
                if l == 0:
                    early(ln_root, -7)
                    at(ln_copy, 0)
                else:
                    at(rec_decay, -3)
                    if i:
                        at(rec_root2, 0)
                    at(rec_square, 6)
                    at(rec_rms, 9)
                if 0 <= j < NT:
                    sims(j)
                for s in range(2):
                    if 0 <= j < NT:
                        row_max(j, s)
                        exps(j, s)
                    if 0 < i < NT:
                        rotate(i, 1 + s)
                if 0 <= j < NT:
                    invert(j, 0)
                    normalise(j, 0)
                if 0 < i < NT:
                    norm_sum(i)
                if i < NT:
                    v_proj(i)
                    keep_v(i)
                if 0 <= n < NT:
                    attend(n)
                if 0 <= m < NT:
                    turn_qk(m)
                at(shift_h2, 8)
                if 0 <= j < NT:
                    invert(j, 1)
                    normalise(j, 1)
                at(square_lo, 10)
                if 0 <= m < NT:
                    keep_k(m)
                    keep_q(m)
                if 0 <= n < NT:
                    keep_o(n)
                if i < NT and not (l and i == 0):
                    add_qk(i)
                    norm_rt(i)
                    scale_qk(i)
                if l:
                    at(rec_a2, -2)
                    if i:
                        at(rec_input, 0)
                if i + 1 < NT:
                    qk_proj(i + 1)
                    square(i + 1)
                if l and i == 0:
                    rec_decay(0)
                    rec_a2(0)
                if l and i == 1:
                    rec_root(0)
                    rec_root2(0)
                    rec_input(0)
                if l and i == 2:
                    rec_scan(0)
                at(square_hc, 9)
                at(mean, 8, i)
                at(proj, 5, i, 0)
                at(proj, 7, i, 1)
                at(var, 10, i)
                at(scale_hc, 11)
                if l == 0:
                    early(ln_stats, -8)
                    early(ln_apply, -7)
                else:
                    at(rec_root, -1)
                    if i > 1:
                        at(rec_scan, 1)
                    at(rec_sum, 7)
                    at(rec_scale, 9)
                if l == 0 and i < 3:
                    set_decay(i)
                if l == 0 and i == 3:
                    avg_r = ve.run(cp(avgr[:], avg[:]), big)
                if i % 4 == 1 and i // 4 + 1 < NB:
                    shift_in(i // 4 + 1)
                if i % 4 == 2 and i // 4 + 1 < NB:
                    shift_rest(i // 4 + 1)
                if i == NT + 1:
                    for q in (sc, ve, po):
                        q.wait(T["tqk", NT - 1], T["add", NT - 1], T["ss", NT - 1])
                    split_hn(0)
                    U["w1"] = split(w1r[:, 0, :], w1r[:, 1, :], w1[:], sc, ve, W["w12", l])[1]
            tail = NT + 3
            barrier(lasts())
            U["g", 0], U["g", 1], U["g", 2] = T["e", NT - 1, 0], T["e", NT - 1, 1], T["PT", NT - 1]
            U["a", 0] = U["a", 1] = T["t2", NT - 1]
            U["a", 2] = T["o", NT - 1]
            if l == 0:
                F["ghalf"] = ve.run(ts(gam[:], gam[:], 0.5, None, ALU.mult), big)
            U["w2"] = split(w2r[:, 0], w2r[:, 1], w2[:], sc, ve, W["w12", l])[1]
            root_var(NB - 2, NT + 2)
            scale_hc(NB - 2)
            for b in range(NB + 3):
                if b + 1 < NB:
                    split_hn(b + 1)
                if b < NB:
                    up(b)
                    if l == 0 and b:
                        conv(b, cv[b % 2])
                if l == 0 and 3 <= b < 6:
                    x = xg[:, 2, :]
                    split_wqkv(b - 3, x, ring[0].start(sp, x, d["wqkv"][:, 1, (b - 3) * 512:(b - 2) * 512], W.get(("wqkv", b - 4)) if b > 3 else None))
                if l == 0 and b == 6:
                    sp.wait(W["wqkv", 2])
                    tabk = set_tables(*load_tables(1, qs))
                if l == 0 and b == NB:
                    pe.wait(U["a", 0], U["a", 1])
                    qk_proj(0)
                if 0 <= b - 1 < NB:
                    if l == 0 and b != 3:
                        gates(b - 1)
                    if l == 0 and b == NB:
                        for q in (sc, ve):
                            q.wait(U["hn", NB - 1], U["a", 2])
                        square(0)
                        for p in range(3):
                            rotate(0, p)
                        norm_sum(0)
                    down(b - 1)
                    if l == 0 and b == 3:
                        gates(b - 1)
                    if l == 0:
                        gates2(b - 1)
                if l == 0 and b == 7:
                    W["w12", 1] = load_w12(1, U["w1"], U["w2"])
                if l == 0 and b == 8:
                    shift_in(0)
                if l == 0 and b == 9:
                    shift_rest(0)
                if l == 0 and b == NB - 1:
                    T = {("h", 0): T["h", 0]}
                if b == 0:
                    proj(NB - 1, tail, 1)
                    proj_add(NB - 1, tail, 1)
                    shift_h2(NB - 1)
                    for q in (sp, ve, po):
                        q.wait(T["wo", NB - 1, 1])
                    if l:
                        rec_sum(NB - 1)
                        st_out = [Dma(sem(f"s_o{i}")) for i in range(2)]
                        for b_ in range(2):
                            xtok[b_] = load_x(b_, xe[b_])
                    else:
                        conv(0, cv[0])
                if b == 1:
                    mean(NB - 1, tail + 1)
                    centre(NB - 1, tail + 1)
                    square_hc(NB - 1)
                    square_lo(NB - 1)
                if b == 2:
                    var(NB - 1, tail + 2)
                    root_var(NB - 1, tail + 2)
                    scale_hc(NB - 1)
                    if l:
                        rec_rms(NB - 1)
                        rec_scale(NB - 1)
                if l and 0 <= b - 2 < NB:
                    end_turn(b - 2)
                    end_out(b - 2)
        last = {i: U["st", NB - 2 + i] for i in range(2)}
        sp.wait(*last.values())

        block = ctx.enter_context(nc.Block())

        @block.tensor
        def _(e):
            pe.emit(e)

        @block.scalar
        def _(e):
            sc.emit(e)

        @block.vector
        def _(e):
            ve.emit(e)

        @block.gpsimd
        def _(e):
            po.emit(e)

        @block.sync
        def _(e):
            sp.emit(e)


def constants():
    f = np.float32
    half = np.arange(0, DH, 2, dtype=f)
    inv = (f(1.0) / np.power(f(10000.0), half / f(DH), dtype=f)).astype(f)
    t = np.arange(L, dtype=f)
    fr = (t[:, None] * inv[None, :]).astype(f)
    fr = np.concatenate([fr, fr], -1).astype(np.float64)
    base = (half + f(0.4 * DH)) / f(1.4 * DH)
    power = (t - f(L // 2)) / f(WIN // 2)
    scale = np.power(base[None, :].astype(np.float64), power[:, None].astype(np.float64))
    scale = np.concatenate([scale, scale], -1)
    cos, sin = np.cos(fr), np.sin(fr)
    sgn = np.concatenate([-np.ones(32), np.ones(32)])[None, :]
    tab = np.stack([np.stack([8 * cos * scale, 8 * sin * scale * sgn], 1),
                    np.stack([cos / scale, sin / scale * sgn], 1)], 0)
    tab = tab.reshape(2, TPB, 128, 2, DH).transpose(2, 0, 1, 3, 4).astype(f)
    q = np.arange(64)[:, None]
    k = np.arange(128)[None, :]
    ok = (k >= q) & (k <= q + 64)
    first = ok & (k >= 64)
    mask = np.zeros((2, 2, 64, 2, 2, 128), f)
    for v in range(2):
        for w in range(2):
            good = first if (v == 0 and w == 0) else ok
            mask[v, :, :, :, w, :] = np.where(good, 0.0, -1e30)[None, :, None, :]
    mask = mask.reshape(2, 128, 512).transpose(1, 0, 2)
    eye = np.eye(128, dtype=f)
    return tab, mask, eye


def kernel(**inputs):
    import ml_dtypes
    import concourse.bacc as bacc
    from concourse.bass_utils import run_bass_kernel_spmd as run

    a = {n.split("_", 2)[2]: np.ascontiguousarray(v) for n, v in inputs.items()}
    tab, mask, eye = constants()
    cols = np.zeros((128, 32), np.float32)
    cols[:, 0], cols[:, 1], cols[:, 2], cols[:, 3] = a["conv_b"], a["b_r"], a["b_i"], a["log_a"]
    cols[:, 4:8] = a["conv_w"][:, 0, :]
    w2 = np.zeros((128, DEPTH, 3, 128), np.float32)
    for l in range(DEPTH):
        c = cols[:, 8 + 9 * l:17 + 9 * l]
        c[:, 0], c[:, 1], c[:, 2] = a["ln_g"][l], a["ln_b"][l], a["b2"][l]
        for j, (o, n) in enumerate(CH):
            c[:n, 3 + j] = a["b1"][l, o:o + n]
            c[:n, 6 + j] = a["b1"][l, HID + o:HID + o + n]
            w2[:n, l, j, :] = a["w2"][l, o:o + n, :]
    feed = {
        "x": a["x"], "cols": cols, "idf": eye, "idb": eye.astype(ml_dtypes.bfloat16),
        "mask": mask.astype(ml_dtypes.bfloat16), "avg": np.full((128, 128), 1.0 / D, np.float32), "tab": tab,
        "wr": np.stack([a["W_r"].T, a["W_i"].T, a["W_out"].T], 1),
        "wqkv": a["wqkv"].transpose(1, 0, 2), "w1": a["w1"].transpose(1, 0, 2), "w2": w2,
        "wo": a["wo"].reshape(DEPTH, 4, 128, 128).transpose(2, 0, 1, 3),
        "gamma": a["gamma"], "q_scale": a["q_scale"], "k_scale": a["k_scale"],
    }
    feed = {n: np.ascontiguousarray(v) for n, v in feed.items()}
    nc = bacc.Bacc("TRN2", target_bir_lowering=False, num_devices=1)
    d = {n: nc.dram_tensor(f"in_{n}", v.shape, mybir.dt.from_np(v.dtype), kind="ExternalInput").ap() for n, v in feed.items()}
    out = nc.dram_tensor("out_0", (NB, L, D), F32, kind="ExternalOutput").ap()
    program(nc, d, out)
    r = run(nc, [{f"in_{n}": v for n, v in feed.items()}], core_ids=[0])
    return r.results[0]["out_0"]
```
